# Optimizing a Trainium2 kernel written in Bass

```python
import numpy as np
import jax
import jax.numpy as jnp

def _softmax(x, axis=-1):
    return jax.nn.softmax(x, axis=axis)

def _gelu(x):
    return jax.nn.gelu(x, approximate=True)

def _silu(x):
    return jax.nn.silu(x)

def _sigmoid(x):
    return jax.nn.sigmoid(x)

def _layernorm(x, axis=-1, eps=1e-05):
    m = jnp.mean(x, axis=axis, keepdims=True)
    v = jnp.var(x, axis=axis, keepdims=True)
    return (x - m) / jnp.sqrt(v + eps)

def _scatter_add(tgt, idx, src, axis=0):
    return tgt.at[idx].add(src)

def _segment_sum(src, seg, n):
    return jax.ops.segment_sum(src, seg, n)
kernel_name = 'mk_lm_tower_d1_tok_ids512_r4_a87ce0'

def setup_inputs(seed: int=0):
    np.random.seed(seed)
    _w = jnp.asarray

    def _rec_inputs():
        import jax
        import jax.numpy as jnp
        _rk = jax.random.key(seed)
        x = jax.random.randint(jax.random.fold_in(_rk, 1), (16, 128), 0, 64, jnp.int32)
        return x
    x = _rec_inputs()

    def _L0_tok_setup():
        import jax, jax.numpy as jnp
        import numpy as np
        NGRAM_SIZES = (2, 3, 4)
        HASH_VOCAB = 25000
        EMBED_DIM = 128
        BATCH, SEQ = (8, 1024)

        def _ngram_hash_ids(byte_sequence, n):
            L = byte_sequence.shape[1] - n + 1
            h = jnp.zeros((byte_sequence.shape[0], L), dtype=jnp.int64)
            for j in range(n):
                h = (h * 64 + byte_sequence[:, j:j + L]) % HASH_VOCAB
            return h

        def _ngram_embed(byte_sequence, table, n):
            B, S = byte_sequence.shape
            ids = _ngram_hash_ids(byte_sequence, n)
            emb = table[ids]
            out = jnp.zeros((B, S, table.shape[1]), dtype=table.dtype)
            c = n // 2
            return out.at[:, c:c + emb.shape[1]].set(emb)
        key = jax.random.key(seed)
        ks = jax.random.split(key, 6)
        return {'byte_sequence': jax.random.randint(ks[0], (BATCH, SEQ), 0, 64, dtype=jnp.int64), 'emb_2': jax.random.normal(ks[1], (HASH_VOCAB, EMBED_DIM), dtype=jnp.float32), 'emb_3': jax.random.normal(ks[2], (HASH_VOCAB, EMBED_DIM), dtype=jnp.float32), 'emb_4': jax.random.normal(ks[3], (HASH_VOCAB, EMBED_DIM), dtype=jnp.float32), 'proj_w': jax.random.normal(ks[4], (EMBED_DIM, len(NGRAM_SIZES) * EMBED_DIM), dtype=jnp.float32) * 0.02, 'proj_b': jax.random.normal(ks[5], (EMBED_DIM,), dtype=jnp.float32) * 0.02}
    _L0_tok_all = _L0_tok_setup()
    _L0_tok_in = {k: v for k, v in _L0_tok_all.items() if k in ('emb_2', 'emb_3', 'emb_4', 'proj_w', 'proj_b')}
    del _L0_tok_all

    def _L0_attn_setup():
        import jax, jax.numpy as jnp
        import numpy as np
        T, B, E, H = (512, 4, 128, 8)
        HD = E // H

        def _rotate_half(x):
            x1, x2 = jnp.split(x, 2, axis=-1)
            return jnp.concatenate([-x2, x1], axis=-1)
        key = jax.random.key(seed)
        ks = jax.random.split(key, 9)
        s = 0.05
        return {'query': jax.random.normal(ks[0], (T, B, E), jnp.float32), 'Wq': jax.random.normal(ks[1], (E, E), jnp.float32) * s, 'bq': jax.random.normal(ks[2], (E,), jnp.float32) * s, 'Wk': jax.random.normal(ks[3], (E, E), jnp.float32) * s, 'bk': jax.random.normal(ks[4], (E,), jnp.float32) * s, 'Wv': jax.random.normal(ks[5], (E, E), jnp.float32) * s, 'bv': jax.random.normal(ks[6], (E,), jnp.float32) * s, 'Wo': jax.random.normal(ks[7], (E, E), jnp.float32) * s, 'bo': jax.random.normal(ks[8], (E,), jnp.float32) * s}
    _L0_attn_all = _L0_attn_setup()
    _L0_attn_in = {k: v for k, v in _L0_attn_all.items() if k in ('Wq', 'bq', 'Wk', 'bk', 'Wv', 'bv', 'Wo', 'bo')}
    del _L0_attn_all

    def _L0_ffn_setup():
        import jax, jax.numpy as jnp
        import numpy as np
        EPS = 1e-06
        SINKHORN_ITERS = 8
        TEMPERATURE = 1.0
        B, N, D = (4, 2048, 128)
        E, OUT = (8, 128)
        H = 1

        def _sinkhorn(logits):
            t = jnp.log(jnp.clip(logits, EPS)) / TEMPERATURE
            for _ in range(SINKHORN_ITERS):
                t = t - jax.nn.logsumexp(t, axis=-2, keepdims=True)
                t = t - jax.nn.logsumexp(t, axis=-1, keepdims=True)
            return jnp.exp(t)
        key = jax.random.key(seed)
        k1, k2, k3 = jax.random.split(key, 3)
        x = jax.random.normal(k1, (B, N, D), dtype=jnp.float32)
        gate_weight = jax.random.normal(k2, (H, D, E), dtype=jnp.float32)
        experts = jax.random.normal(k3, (E, D, OUT), dtype=jnp.float32) * 0.02
        return {'x': x, 'gate_weight': gate_weight, 'experts': experts}
    _L0_ffn_all = _L0_ffn_setup()
    _L0_ffn_in = {k: v for k, v in _L0_ffn_all.items() if k in ('gate_weight', 'experts')}
    del _L0_ffn_all
    return {'x': x, 'L0_tok_emb_2': _L0_tok_in['emb_2'], 'L0_tok_emb_3': _L0_tok_in['emb_3'], 'L0_tok_emb_4': _L0_tok_in['emb_4'], 'L0_tok_proj_w': _L0_tok_in['proj_w'], 'L0_tok_proj_b': _L0_tok_in['proj_b'], 'L0_attn_Wq': _L0_attn_in['Wq'], 'L0_attn_bq': _L0_attn_in['bq'], 'L0_attn_Wk': _L0_attn_in['Wk'], 'L0_attn_bk': _L0_attn_in['bk'], 'L0_attn_Wv': _L0_attn_in['Wv'], 'L0_attn_bv': _L0_attn_in['bv'], 'L0_attn_Wo': _L0_attn_in['Wo'], 'L0_attn_bo': _L0_attn_in['bo'], 'L0_ffn_gate_weight': _L0_ffn_in['gate_weight'], 'L0_ffn_experts': _L0_ffn_in['experts']}

def reference(x, L0_tok_emb_2, L0_tok_emb_3, L0_tok_emb_4, L0_tok_proj_w, L0_tok_proj_b, L0_attn_Wq, L0_attn_bq, L0_attn_Wk, L0_attn_bk, L0_attn_Wv, L0_attn_bv, L0_attn_Wo, L0_attn_bo, L0_ffn_gate_weight, L0_ffn_experts):
    import jax
    import jax.numpy as jnp

    def _L0_tok_ref(byte_sequence, emb_2, emb_3, emb_4, proj_w, proj_b):
        import jax, jax.numpy as jnp
        import numpy as np
        NGRAM_SIZES = (2, 3, 4)
        HASH_VOCAB = 25000
        EMBED_DIM = 128
        BATCH, SEQ = (8, 1024)

        def _ngram_hash_ids(byte_sequence, n):
            L = byte_sequence.shape[1] - n + 1
            h = jnp.zeros((byte_sequence.shape[0], L), dtype=jnp.int64)
            for j in range(n):
                h = (h * 64 + byte_sequence[:, j:j + L]) % HASH_VOCAB
            return h

        def _ngram_embed(byte_sequence, table, n):
            B, S = byte_sequence.shape
            ids = _ngram_hash_ids(byte_sequence, n)
            emb = table[ids]
            out = jnp.zeros((B, S, table.shape[1]), dtype=table.dtype)
            c = n // 2
            return out.at[:, c:c + emb.shape[1]].set(emb)
        tables = (emb_2, emb_3, emb_4)
        combined = jnp.concatenate([_ngram_embed(byte_sequence, t, n) for t, n in zip(tables, NGRAM_SIZES)], axis=-1)
        return jnp.einsum('bsk,dk->bsd', combined, proj_w) + proj_b

    def _L0_attn_ref(query, Wq, bq, Wk, bk, Wv, bv, Wo, bo):
        import jax, jax.numpy as jnp
        import numpy as np
        T, B, E, H = (512, 4, 128, 8)
        HD = E // H

        def _rotate_half(x):
            x1, x2 = jnp.split(x, 2, axis=-1)
            return jnp.concatenate([-x2, x1], axis=-1)
        t_len, bsz, e = query.shape
        scaling = HD ** (-0.5)
        q = (query @ Wq.T + bq) * scaling
        k = query @ Wk.T + bk
        v = query @ Wv.T + bv
        split = lambda x: x.reshape(t_len, bsz * H, HD).transpose(1, 0, 2)
        q, k, v = (split(q), split(k), split(v))
        inv_freq = 1.0 / 10000.0 ** (jnp.arange(0, HD, 2, dtype=jnp.float32) / HD)
        t = jnp.arange(t_len, dtype=jnp.float32)
        freqs = t[:, None] * inv_freq[None, :]
        emb = jnp.concatenate([freqs, freqs], axis=-1)
        cos, sin = (jnp.cos(emb)[None], jnp.sin(emb)[None])
        q = q * cos + _rotate_half(q) * sin
        k = k * cos + _rotate_half(k) * sin
        scores = jnp.einsum('bqd,bkd->bqk', q, k)
        w = jax.nn.softmax(scores.astype(jnp.float32), axis=-1).astype(query.dtype)
        attn = jnp.einsum('bqk,bkd->bqd', w, v)
        attn = attn.transpose(1, 0, 2).reshape(t_len, bsz, e)
        return attn @ Wo.T + bo

    def _L0_ffn_ref(x, gate_weight, experts):
        import jax, jax.numpy as jnp
        import numpy as np
        EPS = 1e-06
        SINKHORN_ITERS = 8
        TEMPERATURE = 1.0
        B, N, D = (4, 2048, 128)
        E, OUT = (8, 128)
        H = 1

        def _sinkhorn(logits):
            t = jnp.log(jnp.clip(logits, EPS)) / TEMPERATURE
            for _ in range(SINKHORN_ITERS):
                t = t - jax.nn.logsumexp(t, axis=-2, keepdims=True)
                t = t - jax.nn.logsumexp(t, axis=-1, keepdims=True)
            return jnp.exp(t)
        b, n, d = x.shape
        e = experts.shape[0]
        m = n // e
        xh = x[:, None, :, :]
        gate_logits = jnp.einsum('bhnd,hde->bhne', xh, gate_weight)
        gates = _sinkhorn(gate_logits)
        g_t = jnp.swapaxes(gates, -1, -2)
        vals, idx = jax.lax.top_k(g_t, m)
        gate_values = jnp.transpose(vals, (2, 0, 1, 3))[..., None]
        routed = jnp.take_along_axis(xh[:, :, None, :, :], idx[..., None], axis=3)
        routed = jnp.transpose(routed, (2, 0, 1, 3, 4))
        expert_w = experts[:, None, :, :]
        outputs = jnp.einsum('ebhmi,ehio->ebhmo', routed, expert_w)
        outputs = outputs * gate_values
        bh_idx = idx.reshape(b, 1, e * m)
        bh_vals = jnp.transpose(outputs, (1, 2, 0, 3, 4)).reshape(b, 1, e * m, outputs.shape[-1])

        def scat(i1, v1):
            return jnp.zeros((n, v1.shape[-1]), dtype=v1.dtype).at[i1].set(v1)
        routed_back = jax.vmap(jax.vmap(scat))(bh_idx, bh_vals)
        return routed_back[:, 0]
    h = _L0_tok_ref(x, L0_tok_emb_2, L0_tok_emb_3, L0_tok_emb_4, L0_tok_proj_w, L0_tok_proj_b)
    h = h + _L0_attn_ref(_layernorm(h, axis=-1), L0_attn_Wq, L0_attn_bq, L0_attn_Wk, L0_attn_bk, L0_attn_Wv, L0_attn_bv, L0_attn_Wo, L0_attn_bo)
    h = h + _L0_ffn_ref(_layernorm(h, axis=-1), L0_ffn_gate_weight, L0_ffn_experts)
    return h

_drawn_inputs = setup_inputs


def setup_inputs(seed=0):
    import zlib

    import numpy as np

    out = dict(_drawn_inputs(seed))
    spreads = {}
    factors = {'L0_attn_bk': 3.614}
    for name, (base, spread) in spreads.items():
        noise = np.random.default_rng([zlib.crc32(name.encode()), seed]).standard_normal(out[name].shape)
        drawn = base * np.exp(spread * noise) if base else spread * noise
        out[name] = jnp.asarray(drawn.astype(out[name].dtype))
    for name, factor in factors.items():
        out[name] = (out[name] * factor).astype(out[name].dtype)
    return out
```

```python
from contextlib import ExitStack

import concourse.bass as bass
from concourse import mybir

F32 = mybir.dt.float32
BF16 = mybir.dt.bfloat16
I32 = mybir.dt.int32
U32 = mybir.dt.uint32
ALU = mybir.AluOpType
ACT = mybir.ActivationFunctionType
AX = mybir.AxisListType

P = 128
T, S, D = 16, 128, 128
H = 8
HD = D // H
NG = 3
VOCAB = 25000
E = 8
CAP = S // E
SUPER = 4
TPS = 4
SPT = P // T
SPS = SPT * TPS
SINKHORN_ITERS = 8
LN_EPS = 1e-5
GATE_EPS = 1e-6
ROUND = float(2 ** 23)
NO_ROW = float(2 ** 20)
PAD = 2

W_PROJ = 0
W_V = W_PROJ + NG * D
W_O = W_V + D
W_Q = W_O + D
W_K = W_Q + D
W_GATE = W_K + D
W_BIAS = W_GATE + E
W_ALL = W_BIAS + 4

C_IDENT = 0
C_SPREAD = C_IDENT + P
C_GROUP = C_SPREAD + 240
C_COS = C_GROUP + 8
C_SIN = C_COS + T
C_ALL_OF_ROW = C_SIN + T
C_ROW_OF = C_ALL_OF_ROW + P
C_LATER = C_ROW_OF + T
C_SLOT = C_LATER + P
C_ALL = C_SLOT + CAP


class Chain:

    def __init__(self, eng, sem, per=0):
        self.eng, self.sem, self.per, self.n = eng, sem, per, 0

    def begin(self):
        self.n = 0

    def step(self, ins, k=0):
        self.n += 1
        ins.then_inc(self.sem, 1)
        self.eng.wait_ge(self.sem, k * self.per + self.n)


def wait_freed(eng, sem, count):
    if not (isinstance(count, int) and count == 0):
        eng.wait_ge(sem, count)


def lm_layer(nc, x_ids, emb_2, emb_3, emb_4, weights, experts, bias_rows, consts, rope, out):
    with ExitStack() as ctx:
        def sb(name, shape, dt=F32):
            return ctx.enter_context(nc.sbuf_tensor(name, shape, dt))

        def sem(name):
            return ctx.enter_context(nc.semaphore(name))

        w_sb = sb("w_sb", [P, W_ALL])
        c_sb = sb("c_sb", [P, C_ALL])
        rope_sb = sb("rope_sb", [P, T, 32])
        later_bf = sb("later_bf", [P, P], BF16)
        exp_sb = sb("exp_sb", [P, E, D])
        brow = sb("brow", [P, 3, D])
        xi = sb("xi", [T, S], I32)
        xf = sb("xf", [T, S + 8])
        hash_all = sb("hash_all", [T, NG, S + SPT + 2])
        hash_v = sb("hash_v", [T, S + 4])
        hash_q = sb("hash_q", [T, S + 4])
        idx_all = sb("idx_all", [P, T, NG], U32)
        emb = sb("emb", [P, TPS, NG, D])
        embT = sb("embT", [P, 2, NG * D])
        h = sb("h", [P, TPS, D])
        hb = sb("hb", [P, T, D])
        xn = sb("xn", [P, TPS, D])
        xnT = sb("xnT", [P, SPS, T])
        wq_rot = sb("wq_rot", [P, T, D])
        wk_rot = sb("wk_rot", [P, T, D])
        b_rot = sb("b_rot", [P, 2, T])
        QT = sb("QT", [P, SPS, T])
        KT = sb("KT", [P, SPS, T])
        V1 = sb("V1", [P, TPS, H, HD + 1])
        Qx = sb("Qx", [P, SPS, H, T])
        smax = sb("smax", [P, SPS])
        prob = sb("prob", [P, SPS, T])
        PT = sb("PT", [P, TPS * H, T])
        Px = sb("Px", [P, TPS * H, SPT, T])
        rden = sb("rden", [P, 2, 2 * H])
        attn = sb("attn", [P, TPS, D])
        attnT = sb("attnT", [P, TPS, D])
        h2 = sb("h2", [P, TPS, D])
        x2 = sb("x2", [P, TPS, D])
        x2T = sb("x2T", [P, T, S])
        stats = [sb(f"stats{n}", [P, TPS, 6]) for n in range(2)]
        mean = [sb(f"mean{n}", [P, TPS]) for n in range(2)]
        mdiff = [sb(f"mdiff{n}", [P, TPS]) for n in range(2)]
        var_eps = [sb(f"var_eps{n}", [P, TPS]) for n in range(2)]
        lnv = [sb(f"lnv{n}", [P, TPS]) for n in range(2)]
        rstd0 = [sb(f"rstd0{n}", [P, TPS]) for n in range(2)]
        nwt = [sb(f"nwt{n}", [P, TPS]) for n in range(2)]
        rstd = [sb(f"rstd{n}", [P, TPS]) for n in range(2)]
        x2s = sb("x2s", [P, T, D])
        h2s = sb("h2s", [P, T, D])
        KA = sb("KA", [P, P])
        KB = sb("KB", [P, P])
        R = sb("R", [P, T])
        Cj = sb("Cj", [P, T])
        cdiag = sb("cdiag", [P, T])
        csum = sb("csum", [P, 1])
        cinv = sb("cinv", [P, 1])
        scaled = sb("scaled", [P, P])
        rinv = sb("rinv", [P, P])
        G = sb("G", [P, P])
        G1 = sb("G1", [P, P])
        G2 = sb("G2", [P, P])
        top = sb("top", [P, 2, 8])
        M_bf = sb("M_bf", [P, P], BF16)
        win = sb("win", [P, P])
        pos = sb("pos", [P, P])
        slot = sb("slot", [P, P])
        wgate = sb("wgate", [P, P])
        slotT = sb("slotT", [P, P])
        gate_tok = sb("gate_tok", [P, T])
        onehot = sb("onehot", [P, T, E, CAP])
        onehotT = sb("onehotT", [P, 2, 4, S])
        xg = sb("xg", [P, 2, E, 4, CAP])
        yT = sb("yT", [P, 2, 4, E, CAP])
        y = sb("y", [P, 2, 4, D])
        res = sb("res", [P, T, D])

        bank = [ctx.enter_context(nc.psum_tensor(f"bank{n}", [P, 512], F32)) for n in range(8)]

        h2_dram = nc.dram_tensor("h2_scratch", (S * T, D), F32, kind="Internal").ap()
        x2_dram = nc.dram_tensor("x2_scratch", (S * T, D), F32, kind="Internal").ap()

        ident = c_sb[:, C_IDENT:C_IDENT + P]
        group = c_sb[:, C_GROUP:C_GROUP + 8]
        row_of = c_sb[:, C_ROW_OF:C_ROW_OF + T]
        all_of_row = c_sb[:, C_ALL_OF_ROW:C_ALL_OF_ROW + P]
        slot_no = c_sb[:, C_SLOT:C_SLOT + CAP]

        x_in, c_in, w_in, rope_in, exp_in, brow_in = (sem(n) for n in
                                                      ("x_in", "c_in", "w_in", "rope_in", "exp_in", "brow_in"))
        ids_step, hashed, spread, idx_ready = (sem(n) for n in ("ids_step", "hashed", "spread", "idx_ready"))
        emb_cleared = sem("emb_cleared")
        gathered = [sem(f"gathered{n}") for n in range(TPS)]
        rope_mm, rope_copied_v, rope_copied_a, brot_step, setup_step = (
            sem(n) for n in ("rope_mm", "rope_copied_v", "rope_copied_a", "brot_step", "setup_step"))
        embT_done, embT_copied, proj_done = sem("embT_done"), sem("embT_copied"), sem("proj_done")
        a_step, b_step = sem("a_step"), sem("b_step")
        h_ready, hb_done = sem("h_ready"), sem("hb_done")
        var_ready = [sem("var1_ready"), sem("var2_ready")]
        ln_log = [sem("ln1_log"), sem("ln2_log")]
        rstd0_ready = [sem("rstd1_guess"), sem("rstd2_guess")]
        xn_ready, xnT_done, xnT_copied = sem("xn_ready"), sem("xnT_done"), sem("xnT_copied")
        q_done, k_done, v_done = sem("q_done"), sem("k_done"), sem("v_done")
        q_ready, k_ready, v_ready = sem("q_ready"), sem("k_ready"), sem("v_ready")
        qx_v, qx_a = sem("qx_v"), sem("qx_a")
        scores_done, shifted, probs_ready = sem("scores_done"), sem("shifted"), sem("probs_ready")
        PT_done, PT_copied, px_v, px_a = sem("PT_done"), sem("PT_copied"), sem("px_v"), sem("px_a")
        pv_done, attn_ready, attnT_done, attnT_copied = (
            sem(n) for n in ("pv_done", "attn_ready", "attnT_done", "attnT_copied"))
        wo_done, h2_ready, x2_ready, x2T_done, x2T_copied = (
            sem(n) for n in ("wo_done", "h2_ready", "x2_ready", "x2T_done", "x2T_copied"))
        h2_stored, x2_stored, h2s_in, x2s_in = (sem(n) for n in ("h2_stored", "x2_stored", "h2s_in", "x2s_in"))
        logits_done, ka_ready, kaT_done, kb_ready = (
            sem(n) for n in ("logits_done", "ka_ready", "kaT_done", "kb_ready"))
        r_ready, colsum_done, c_ready, rowsum_done, sink_step = (
            sem(n) for n in ("r_ready", "colsum_done", "c_ready", "rowsum_done", "sink_step"))
        scaled_ready, rowsumB_done, top_step, m_ready, later_done = (
            sem(n) for n in ("scaled_ready", "rowsumB_done", "top_step", "m_ready", "later_done"))
        slot_ready, wg_ready, slotT_done, onehot_ready = (
            sem(n) for n in ("slot_ready", "wg_ready", "slotT_done", "onehot_ready"))
        xg_done, xg_copied, ohT_done, ohT_copied = (
            sem(n) for n in ("xg_done", "xg_copied", "ohT_done", "ohT_copied"))
        yT_done, yT_copied, y_done, y_copied, scat_done, res_ready = (
            sem(n) for n in ("yT_done", "yT_copied", "y_done", "y_copied", "scat_done", "res_ready"))
        out_stored = sem("out_stored")

        MASKS_V = 5
        CHUNK = 4
        NCH = T // CHUNK

        block = ctx.enter_context(nc.Block())

        @block.sync
        def _(sp):
            sp.dma_start(xi[:, :], x_ids).then_inc(x_in, 16)
            sp.dma_start(c_sb[:, :], consts).then_inc(c_in, 16)
            sp.dma_start(w_sb[:, :], weights).then_inc(w_in, 16)
            sp.dma_start(rope_sb[:, :, :], rope).then_inc(rope_in, 16)
            sp.dma_start(brow[:, :, :], bias_rows.partition_broadcast(P)).then_inc(brow_in, 16)
            sp.dma_start(exp_sb[:, :, :], experts).then_inc(exp_in, 16)

            def store(k):
                rows = slice(k * TPS * P, (k + 1) * TPS * P) if isinstance(k, int) else bass.ds(k * (TPS * P), TPS * P)
                sp.wait_ge(h2_ready, k + 1)
                sp.dma_start(h2_dram[rows, :].rearrange("(i p) d -> p i d", p=P), h2[:, :, :]).then_inc(h2_stored, 16)
                sp.wait_ge(x2_ready, k + 1)
                sp.dma_start(x2_dram[rows, :].rearrange("(i p) d -> p i d", p=P), x2[:, :, :]).then_inc(x2_stored, 16)

            with sp.Fori(0, SUPER) as k:
                store(k)
            sp.wait_ge(x2_stored, 16 * SUPER)
            sp.dma_start(x2s[:, :, :], x2_dram.rearrange("(s t) d -> s t d", t=T)).then_inc(x2s_in, 16)
            sp.wait_ge(h2_stored, 16 * SUPER)
            sp.dma_start(h2s[:, :, :], h2_dram.rearrange("(s t) d -> s t d", t=T)).then_inc(h2s_in, 16)
            for c in range(NCH):
                sp.wait_ge(res_ready, c + 1)
                sp.dma_start(out[c * CHUNK:(c + 1) * CHUNK, :, :].rearrange("b s d -> s b d"),
                             res[:, c * CHUNK:(c + 1) * CHUNK, :]).then_inc(out_stored, 16)
            sp.wait_ge(out_stored, 16 * NCH)

        @block.gpsimd
        def _(pool):
            tables = (emb_2, emb_3, emb_4)

            def gather(k):
                for i in range(TPS):
                    if k > 0:
                        pool.wait_ge(embT_done, TPS * (k - 1) + i + 1)
                    tile = k * TPS + i
                    if tile in (0, T - 1):
                        pool.memset(emb[:, i, :, :], 0.0).then_inc(emb_cleared, 1)
                        pool.wait_ge(emb_cleared, 1 if tile == 0 else 2)
                    for n in range(NG):
                        pool.indirect_dma_start(
                            emb[:, i, n, :], None, tables[n],
                            bass.IndirectOffsetOnAxis(ap=idx_all[:, tile, n:n + 1], axis=0),
                            bounds_check=VOCAB - 1, oob_is_err=False).then_inc(gathered[i], 16)

            def add_bo(k):
                pool.wait_ge(h_ready, k + 1)
                pool.tensor_tensor(hb[:, k * TPS:(k + 1) * TPS, :], h[:, :, :],
                                   brow[:, 2:3, :].to_broadcast([P, TPS, D]), ALU.add).then_inc(hb_done, 1)

            pool.wait_ge(idx_ready, 1)
            gather(0)
            pool.wait_ge(brow_in, 16)
            for k in range(1, SUPER):
                gather(k)
                add_bo(k - 1)
            add_bo(SUPER - 1)

        @block.scalar
        def _(act):
            def guess_rstd(n, k):
                act.wait_ge(var_ready[n], k + 1)
                act.activation(lnv[n][:, :], var_eps[n][:, :], ACT.Ln).then_inc(ln_log[n], 1)
                act.wait_ge(ln_log[n], k + 1)
                act.activation(rstd0[n][:, :], lnv[n][:, :], ACT.Exp, scale=-0.5).then_inc(rstd0_ready[n], 1)

            def copy_embT(k, tiles):
                for i in tiles:
                    act.wait_ge(embT_done, k * TPS + i + 1)
                    if not (isinstance(k, int) and k == 0 and i < 2):
                        act.wait_ge(proj_done, k * TPS + i - 1)
                    act.activation(embT[:, i % 2, :], bank[i % 2][:, 0:NG * D], ACT.Copy).then_inc(embT_copied, 1)

            def copy_xnT(k):
                act.wait_ge(xnT_done, k + 1)
                wait_freed(act, v_done, k)
                act.activation(xnT[:, :, :], bank[2][:, :].rearrange("p (s t) -> p s t", t=T),
                               ACT.Copy).then_inc(xnT_copied, 1)

            def mask_q(k):
                act.wait_ge(q_ready, k + 1)
                wait_freed(act, scores_done, k)
                for g in range(MASKS_V, H):
                    ins = act.activation(Qx[:, :, g, :], QT[:, :, :], ACT.Copy, scale=group[:, g:g + 1])
                ins.then_inc(qx_a, 1)

            def exps(k):
                act.wait_ge(shifted, k + 1)
                act.activation(prob[:, :, :], prob[:, :, :], ACT.Exp).then_inc(probs_ready, 1)

            def copy_PT(k):
                act.wait_ge(PT_done, k + 1)
                wait_freed(act, px_v, k)
                act.activation(PT[:, :, :], bank[6][:, :].rearrange("p (a t) -> p a t", t=T), ACT.Copy).then_inc(PT_copied, 1)

            def mask_p(k):
                act.wait_ge(PT_copied, k + 1)
                for g in range(MASKS_V, SPT):
                    ins = act.activation(Px[:, :, g, :], PT[:, :, :], ACT.Copy, scale=group[:, g:g + 1])
                ins.then_inc(px_a, 1)

            def copy_attnT(k):
                act.wait_ge(attnT_done, k + 1)
                act.activation(attnT[:, :, :], bank[7][:, :].rearrange("p (i d) -> p i d", d=D), ACT.Copy).then_inc(attnT_copied, 1)

            def copy_x2T(k):
                act.wait_ge(x2T_done, k + 1)
                dst = x2T[:, :, k * SPS:(k + 1) * SPS] if isinstance(k, int) else x2T[:, :, bass.ds(k * SPS, SPS)]
                act.activation(dst.rearrange("p t s -> p s t"), bank[3][:, :].rearrange("p (s t) -> p s t", t=T),
                               ACT.Copy).then_inc(x2T_copied, 1)

            for j in range(4):
                act.wait_ge(rope_mm, 5 + j)
                act.activation(wk_rot[:, :, 32 * j:32 * j + 32], bank[4 + j][:, :].rearrange("p (t c) -> p t c", c=32),
                               ACT.Copy).then_inc(rope_copied_a, 1)
            copy_embT(0, range(TPS))
            guess_rstd(0, 0)
            copy_xnT(0)

            def attention(k, more):
                if more:
                    copy_embT(k + 1, (0, 1))
                mask_q(k)
                if more:
                    copy_embT(k + 1, (2, 3))
                    guess_rstd(0, k + 1)
                exps(k)
                copy_PT(k)
                mask_p(k)
                if more:
                    copy_xnT(k + 1)
                copy_attnT(k)
                guess_rstd(1, k)
                copy_x2T(k)

            attention(0, True)
            with act.Fori(1, SUPER - 1) as k:
                attention(k, True)
            attention(SUPER - 1, False)

            for c in range(NCH):
                act.wait_ge(xg_done, c + 1)
                if c >= 2:
                    act.wait_ge(yT_done, c - 1)
                act.activation(xg[:, c % 2, :, :, :].rearrange("p e b j -> p b e j"),
                               bank[0][:, :].rearrange("p (b e j) -> p b e j", b=CHUNK, e=E), ACT.Copy).then_inc(xg_copied, 1)
                act.wait_ge(yT_done, c + 1)
                act.activation(yT[:, c % 2, :, :, :].rearrange("p b e j -> p e b j"),
                               bank[2][:, :].rearrange("p (e b j) -> p e b j", b=CHUNK, e=E), ACT.Copy).then_inc(yT_copied, 1)
                act.wait_ge(y_done, c + 1)
                act.activation(y[:, c % 2, :, :], bank[3][:, :].rearrange("p (b d) -> p b d", b=CHUNK),
                               ACT.Copy).then_inc(y_copied, 1)

        @block.tensor
        def _(pe):
            pe.wait_ge(c_in, 16)
            pe.wait_ge(hashed, 1)
            for s in range(SPT):
                at = C_SPREAD + T * (SPT - 1) - T * s
                ins = pe.matmul(bank[0][:, 0:NG * T], c_sb[0:T, at:at + P], hash_all[:, :, 1 + s:1 + s + S:SPT],
                                start=(s == 0), stop=(s == SPT - 1))
            ins.then_inc(spread, 1)
            pe.wait_ge(w_in, 16)
            pe.wait_ge(rope_in, 16)
            for n, w0 in enumerate((W_Q, W_K)):
                for j in range(4):
                    if n == 1:
                        pe.wait_ge(rope_copied_v, j + 1)
                    pe.matmul(bank[4 + j][:, :], w_sb[32 * j:32 * j + 32, w0:w0 + D],
                              rope_sb[32 * j:32 * j + 32, :, :], start=True, stop=True).then_inc(rope_mm, 1)

            def embed(k, tiles):
                for i in tiles:
                    pe.wait_ge(gathered[i], (k + 1) * (16 * NG))
                    if isinstance(k, int) and k == 0 and i < 2:
                        pe.wait_ge(idx_ready, 1)
                    else:
                        pe.wait_ge(embT_copied, k * TPS + i - 1)
                    for n in range(NG):
                        ins = pe.transpose(bank[i % 2][:, n * D:(n + 1) * D], emb[:, i, n, :], ident)
                    ins.then_inc(embT_done, 1)
                    if i == 0:
                        wait_freed(pe, xnT_copied, k)
                    pe.wait_ge(embT_copied, k * TPS + i + 1)
                    for n in range(NG):
                        ins = pe.matmul(bank[2][:, i * D:(i + 1) * D], embT[:, i % 2, n * D:(n + 1) * D],
                                        w_sb[:, W_PROJ + n * D:W_PROJ + (n + 1) * D], start=(n == 0), stop=(n == NG - 1))
                    ins.then_inc(proj_done, 1)

            def transpose_xn(k):
                pe.wait_ge(xn_ready, k + 1)
                for i in range(TPS):
                    ins = pe.transpose(bank[2][:, i * D:(i + 1) * D], xn[:, i, :], ident)
                ins.then_inc(xnT_done, 1)

            def qkv(k):
                pe.wait_ge(xnT_copied, k + 1)
                wait_freed(pe, attn_ready, k)
                for b, w, done in ((4, wq_rot, q_done), (5, wk_rot, k_done)):
                    for t in range(T):
                        ins = pe.matmul(bank[b][:, t * SPS:(t + 1) * SPS], w[:, t, :], xnT[:, :, t], start=True, stop=True)
                    ins.then_inc(done, 1)
                wait_freed(pe, PT_copied, k)
                for i in range(TPS):
                    ins = pe.matmul(bank[6][:, i * D:(i + 1) * D],
                                    xnT[:, i * SPT:(i + 1) * SPT, :].rearrange("p s t -> p (s t)"),
                                    w_sb[:, W_V:W_V + D], start=True, stop=True)
                ins.then_inc(v_done, 1)

            def scores(k):
                pe.wait_ge(k_ready, k + 1)
                pe.wait_ge(qx_v, k + 1)
                pe.wait_ge(qx_a, k + 1)
                wait_freed(pe, attnT_copied, k)
                for s in range(SPS):
                    ins = pe.matmul(bank[7][:, s * T:(s + 1) * T], Qx[:, s, :, :], KT[:, s, :], start=True, stop=True)
                ins.then_inc(scores_done, 1)

            def transpose_prob(k):
                pe.wait_ge(probs_ready, k + 1)
                pe.wait_ge(v_ready, k + 1)
                for i in range(TPS):
                    ins = pe.transpose(bank[6][:, i * P:(i + 1) * P],
                                       prob[:, i * SPT:(i + 1) * SPT, :].rearrange("p s t -> p (s t)"), ident)
                ins.then_inc(PT_done, 1)

            def weigh_v(k):
                pe.wait_ge(px_v, k + 1)
                pe.wait_ge(px_a, k + 1)
                for i in range(TPS):
                    for g in range(H):
                        at = ((i % 2) * H + g) * (HD + 1)
                        ins = pe.matmul(bank[4 + i // 2][:, at:at + HD + 1], Px[:, i * H + g, :, :], V1[:, i, g, :],
                                        start=True, stop=True)
                ins.then_inc(pv_done, 1)

            def project_out(k):
                pe.wait_ge(attn_ready, k + 1)
                for i in range(TPS):
                    ins = pe.transpose(bank[7][:, i * D:(i + 1) * D], attn[:, i, :], ident)
                ins.then_inc(attnT_done, 1)
                pe.wait_ge(attnT_copied, k + 1)
                wait_freed(pe, x2T_copied, k)
                for i in range(TPS):
                    ins = pe.matmul(bank[3][:, i * D:(i + 1) * D], attnT[:, i, :], w_sb[:, W_O:W_O + D],
                                    start=True, stop=True)
                ins.then_inc(wo_done, 1)

            def transpose_x2(k):
                pe.wait_ge(x2_ready, k + 1)
                for i in range(TPS):
                    ins = pe.transpose(bank[3][:, i * D:(i + 1) * D], x2[:, i, :], ident)
                ins.then_inc(x2T_done, 1)

            embed(0, range(TPS))
            transpose_xn(0)
            pe.wait_ge(rope_copied_v, 4)
            pe.wait_ge(rope_copied_a, 4)

            def attention(k, more):
                qkv(k)
                if more:
                    embed(k + 1, (0, 1))
                scores(k)
                if more:
                    embed(k + 1, (2, 3))
                transpose_prob(k)
                weigh_v(k)
                if more:
                    transpose_xn(k + 1)
                project_out(k)
                transpose_x2(k)

            attention(0, True)
            with pe.Fori(1, SUPER - 1) as k:
                attention(k, True)
            attention(SUPER - 1, False)

            pe.wait_ge(x2T_copied, SUPER)
            for b in range(T):
                ins = pe.matmul(bank[0][:, b * E:(b + 1) * E], x2T[:, b, :], w_sb[:, W_GATE:W_GATE + E], start=True, stop=True)
            ins.then_inc(logits_done, 1)
            pe.wait_ge(ka_ready, 1)
            pe.transpose(bank[1][:, 0:P], KA[:, :], ident).then_inc(kaT_done, 1)
            pe.wait_ge(r_ready, 1)
            with pe.Fori(0, SINKHORN_ITERS - 1) as n:
                pe.wait_ge(r_ready, n + 1)
                pe.matmul(bank[2][:, 0:T], KA[:, :], R[:, :], start=True, stop=True).then_inc(colsum_done, 1)
                pe.wait_ge(c_ready, n + 1)
                pe.matmul(bank[3][:, 0:T], KB[:, :], Cj[:, :], start=True, stop=True).then_inc(rowsum_done, 1)
            pe.wait_ge(r_ready, SINKHORN_ITERS)
            pe.matmul(bank[2][:, 0:T], KA[:, :], R[:, :], start=True, stop=True).then_inc(colsum_done, 1)
            pe.wait_ge(scaled_ready, 1)
            pe.matmul(bank[3][:, 0:P], scaled[:, :], KB[:, :], start=True, stop=True).then_inc(rowsumB_done, 1)
            pe.wait_ge(m_ready, 1)
            pe.matmul(bank[4][:, 0:P], later_bf[:, :], M_bf[:, :], start=True, stop=True).then_inc(later_done, 1)
            pe.wait_ge(slot_ready, 1)
            pe.transpose(bank[5][:, 0:P], slot[:, :], ident).then_inc(slotT_done, 1)
            pe.wait_ge(wg_ready, 1)
            pe.transpose(bank[6][:, 0:P], wgate[:, :], ident).then_inc(slotT_done, 1)

            pe.wait_ge(x2s_in, 16)
            pe.wait_ge(exp_in, 16)
            for c in range(NCH):
                pe.wait_ge(onehot_ready, c + 1)
                if c >= 1:
                    pe.wait_ge(xg_copied, c)
                for b in range(CHUNK):
                    ins = pe.matmul(bank[0][:, b * P:(b + 1) * P], x2s[:, c * CHUNK + b, :],
                                    onehot[:, c * CHUNK + b, :, :], start=True, stop=True)
                ins.then_inc(xg_done, 1)
                if c >= 1:
                    pe.wait_ge(ohT_copied, c)
                for b in range(CHUNK):
                    ins = pe.transpose(bank[1][:, b * P:(b + 1) * P],
                                       onehot[:, c * CHUNK + b, :, :].rearrange("p e j -> p (e j)"), ident)
                ins.then_inc(ohT_done, 1)
                pe.wait_ge(xg_copied, c + 1)
                if c >= 1:
                    pe.wait_ge(yT_copied, c)
                for e in range(E):
                    w = CHUNK * CAP
                    ins = pe.matmul(bank[2][:, e * w:(e + 1) * w], exp_sb[:, e, :], xg[:, c % 2, e, :, :],
                                    start=True, stop=True)
                ins.then_inc(yT_done, 1)
                pe.wait_ge(yT_copied, c + 1)
                if c >= 1:
                    pe.wait_ge(y_copied, c)
                for b in range(CHUNK):
                    ins = pe.transpose(bank[3][:, b * P:(b + 1) * P],
                                       yT[:, c % 2, b, :, :].rearrange("p e j -> p (e j)"), ident)
                ins.then_inc(y_done, 1)
                pe.wait_ge(y_copied, c + 1)
                pe.wait_ge(ohT_copied, c + 1)
                if c >= 1:
                    pe.wait_ge(res_ready, c)
                for b in range(CHUNK):
                    ins = pe.matmul(bank[4][:, b * D:(b + 1) * D], onehotT[:, c % 2, b, :], y[:, c % 2, b, :],
                                    start=True, stop=True)
                ins.then_inc(scat_done, 1)

        @block.vector
        def _(dve):
            ids = Chain(dve, ids_step)
            W = S + PAD
            v, q = hash_v[:, 0:W], hash_q[:, 0:W]

            def mod_vocab(dst):
                ids.step(dve.tensor_scalar(q, v, 1.0 / VOCAB, ROUND, ALU.mult, ALU.add))
                ids.step(dve.tensor_scalar(q, q, -ROUND, -float(VOCAB), ALU.add, ALU.mult))
                ids.step(dve.tensor_tensor(v, v, q, ALU.add))
                ids.step(dve.tensor_scalar(q, v, 0.0, float(VOCAB), ALU.is_lt, ALU.mult))
                ids.step(dve.tensor_tensor(dst, v, q, ALU.add))

            dve.memset(xf[:, :], 0.0).then_inc(ids_step, 1)
            ids.n += 1
            ids.step(dve.memset(hash_all[:, :, :], 0.0))
            dve.wait_ge(x_in, 16)
            ids.step(dve.tensor_copy(xf[:, PAD:PAD + S], xi[:, :]))
            h2g, h3g, h4g = hash_all[:, 0, 0:W], hash_all[:, 1, 0:W], hash_all[:, 2, 1:1 + W]
            ids.step(dve.scalar_tensor_tensor(v, xf[:, 0:W], 64.0, xf[:, 1:1 + W], ALU.mult, ALU.add))
            mod_vocab(h2g)
            ids.step(dve.scalar_tensor_tensor(v, h2g, 64.0, xf[:, 2:2 + W], ALU.mult, ALU.add))
            mod_vocab(h3g)
            ids.step(dve.scalar_tensor_tensor(v, h3g, 64.0, xf[:, 3:3 + W], ALU.mult, ALU.add))
            mod_vocab(h4g)
            ids.step(dve.memset(hash_all[:, :, 1:2], NO_ROW))
            ids.step(dve.memset(hash_all[:, 1:3, S:S + 1], NO_ROW))
            dve.memset(hash_all[:, 2, 2:3], NO_ROW).then_inc(hashed, 1)
            dve.wait_ge(spread, 1)
            dve.tensor_copy(idx_all[:, :, :].rearrange("p i n -> p n i"),
                            bank[0][:, 0:NG * T].rearrange("p (n i) -> p n i", n=NG)).then_inc(idx_ready, 1)

            for j in range(4):
                dve.wait_ge(rope_mm, 1 + j)
                dve.tensor_scalar(wq_rot[:, :, 32 * j:32 * j + 32], bank[4 + j][:, :].rearrange("p (t c) -> p t c", c=32),
                                  HD ** -0.5, None, ALU.mult).then_inc(rope_copied_v, 1)
            setup = Chain(dve, setup_step)
            for n, scale in ((0, HD ** -0.5), (1, 1.0)):
                setup.step(dve.tensor_scalar(b_rot[:, n, :], c_sb[:, C_COS:C_COS + T],
                                             w_sb[:, W_BIAS + n:W_BIAS + n + 1], None, ALU.mult))
                setup.step(dve.scalar_tensor_tensor(b_rot[:, n, :], c_sb[:, C_SIN:C_SIN + T],
                                                    w_sb[:, W_BIAS + 2 + n:W_BIAS + 3 + n], b_rot[:, n, :],
                                                    ALU.mult, ALU.add))
                if scale != 1.0:
                    setup.step(dve.tensor_scalar(b_rot[:, n, :], b_rot[:, n, :], scale, None, ALU.mult))
            setup.step(dve.memset(V1[:, :, :, HD:HD + 1], 1.0))
            setup.step(dve.tensor_copy(later_bf[:, :], c_sb[:, C_LATER:C_LATER + P]))
            dve.wait_ge(brow_in, 16)

            def layernorm(n, k, chain, src, dst, ready, before=None):
                for i in range(TPS):
                    ins = dve.bn_stats(stats[n][:, i, :], src[:, i, :])
                chain.step(ins, k)
                even, odd = stats[n][:, :, 1], stats[n][:, :, 4]
                dve.tensor_tensor(mean[n][:, :], even, odd, ALU.add)
                dve.tensor_tensor(mdiff[n][:, :], even, odd, ALU.subtract)
                chain.step(dve.tensor_tensor(var_eps[n][:, :], stats[n][:, :, 2], stats[n][:, :, 5], ALU.add), k)
                dve.tensor_scalar(mean[n][:, :], mean[n][:, :], 0.5, None, ALU.mult)
                dve.tensor_scalar(var_eps[n][:, :], var_eps[n][:, :], 1.0 / D, LN_EPS, ALU.mult, ALU.add)
                chain.step(dve.scalar_tensor_tensor(mdiff[n][:, :], mdiff[n][:, :], 0.25, mdiff[n][:, :],
                                                    ALU.mult, ALU.mult), k)
                dve.tensor_tensor(var_eps[n][:, :], var_eps[n][:, :], mdiff[n][:, :], ALU.add).then_inc(var_ready[n], 1)
                dve.wait_ge(rstd0_ready[n], k + 1)
                chain.step(dve.tensor_tensor(nwt[n][:, :], rstd0[n][:, :], rstd0[n][:, :], ALU.mult), k)
                chain.step(dve.tensor_tensor(nwt[n][:, :], nwt[n][:, :], var_eps[n][:, :], ALU.mult), k)
                chain.step(dve.tensor_scalar(nwt[n][:, :], nwt[n][:, :], -0.5, 1.5, ALU.mult, ALU.add), k)
                chain.step(dve.tensor_tensor(rstd[n][:, :], nwt[n][:, :], rstd0[n][:, :], ALU.mult), k)
                for i in range(TPS):
                    ins = dve.tensor_scalar(dst[:, i, :], src[:, i, :], mean[n][:, i:i + 1], rstd[n][:, i:i + 1],
                                            ALU.subtract, ALU.mult)
                ins.then_inc(ready, 1)

            ach = Chain(dve, a_step, per=7)
            bch = Chain(dve, b_step, per=9)

            def embed(k):
                dve.wait_ge(proj_done, TPS * (k + 1))
                wait_freed(dve, hb_done, k)
                dve.tensor_tensor(h[:, :, :], bank[2][:, :].rearrange("p (i d) -> p i d", d=D),
                                  brow[:, 0:1, :].to_broadcast([P, TPS, D]), ALU.add).then_inc(h_ready, 1)
                dve.wait_ge(h_ready, k + 1)
                ach.begin()
                layernorm(0, k, ach, h, xn, xn_ready)
                assert ach.n == ach.per

            def take_qk(k):
                dve.wait_ge(q_done, k + 1)
                wait_freed(dve, qx_a, k)
                for b, n, dst, ready in ((4, 0, QT, q_ready), (5, 1, KT, k_ready)):
                    if n == 1:
                        dve.wait_ge(k_done, k + 1)
                        wait_freed(dve, scores_done, k)
                    dve.tensor_tensor(dst[:, :, :].rearrange("p s t -> p t s"),
                                      bank[b][:, :].rearrange("p (t s) -> p t s", t=T),
                                      b_rot[:, n, :].unsqueeze(2).to_broadcast([P, T, SPS]), ALU.add).then_inc(ready, 1)
                dve.wait_ge(q_ready, k + 1)
                for g in range(MASKS_V):
                    ins = dve.tensor_scalar(Qx[:, :, g, :], QT[:, :, :], group[:, g:g + 1], None, ALU.mult)
                ins.then_inc(qx_v, 1)
                dve.wait_ge(v_done, k + 1)
                wait_freed(dve, pv_done, k)
                dve.tensor_tensor(V1[:, :, :, 0:HD], bank[6][:, :].rearrange("p (i g d) -> p i g d", i=TPS, d=HD),
                                  brow[:, 1, :].rearrange("p (g d) -> p g d", d=HD).unsqueeze(1).to_broadcast([P, TPS, H, HD]),
                                  ALU.add).then_inc(v_ready, 1)

            def shift(k):
                dve.wait_ge(scores_done, k + 1)
                sc = bank[7][:, :].rearrange("p (s t) -> p s t", t=T)
                bch.step(dve.tensor_reduce(smax[:, :], sc, AX.X, ALU.max), k)
                dve.tensor_tensor(prob[:, :, :], sc, smax[:, :].unsqueeze(2).to_broadcast([P, SPS, T]),
                                  ALU.subtract).then_inc(shifted, 1)

            def mask_p(k):
                dve.wait_ge(PT_copied, k + 1)
                for g in range(MASKS_V):
                    ins = dve.tensor_scalar(Px[:, :, g, :], PT[:, :, :], group[:, g:g + 1], None, ALU.mult)
                ins.then_inc(px_v, 1)

            def normalise(k):
                dve.wait_ge(pv_done, k + 1)
                for n in range(2):
                    o = bank[4 + n][:, 0:2 * H * (HD + 1)].rearrange("p (a d) -> p a d", d=HD + 1)
                    ins = dve.reciprocal(rden[:, n, :], o[:, :, HD])
                bch.step(ins, k)
                for n in range(2):
                    o = bank[4 + n][:, 0:2 * H * (HD + 1)].rearrange("p (a d) -> p a d", d=HD + 1)
                    ins = dve.tensor_tensor(attn[:, 2 * n:2 * n + 2, :].rearrange("p i (g d) -> p (i g) d", d=HD),
                                            o[:, :, 0:HD], rden[:, n, :].unsqueeze(2).to_broadcast([P, 2 * H, HD]), ALU.mult)
                ins.then_inc(attn_ready, 1)

            def residual(k):
                dve.wait_ge(wo_done, k + 1)
                dve.wait_ge(hb_done, k + 1)
                wait_freed(dve, h2_stored, k * 16)
                wait_freed(dve, x2_stored, k * 16)
                src = hb[:, k * TPS:(k + 1) * TPS, :] if isinstance(k, int) else hb[:, bass.ds(k * TPS, TPS), :]
                dve.tensor_tensor(h2[:, :, :], bank[3][:, :].rearrange("p (i d) -> p i d", d=D), src,
                                  ALU.add).then_inc(h2_ready, 1)
                dve.wait_ge(h2_ready, k + 1)
                layernorm(1, k, bch, h2, x2, x2_ready)

            embed(0)

            def attention(k, more):
                bch.begin()
                take_qk(k)
                shift(k)
                if more:
                    embed(k + 1)
                mask_p(k)
                normalise(k)
                residual(k)
                assert bch.n == bch.per

            attention(0, True)
            with dve.Fori(1, SUPER - 1) as k:
                attention(k, True)
            attention(SUPER - 1, False)

            sink = Chain(dve, sink_step, per=2)
            dve.memset(R[:, :], 1.0).then_inc(r_ready, 1)
            dve.wait_ge(logits_done, 1)
            dve.tensor_scalar(KA[:, :], bank[0][:, 0:P], GATE_EPS, None, ALU.max).then_inc(ka_ready, 1)
            dve.wait_ge(kaT_done, 1)
            dve.tensor_copy(KB[:, :], bank[1][:, 0:P]).then_inc(kb_ready, 1)
            dve.wait_ge(kb_ready, 1)

            def columns(n):
                sink.begin()
                dve.wait_ge(colsum_done, n + 1)
                sink.step(dve.scalar_tensor_tensor(cdiag[:, :], bank[2][:, 0:T], 1.0, row_of, ALU.mult, ALU.mult,
                                                   accum_out=csum[:, :]), n)
                sink.step(dve.reciprocal(cinv[:, :], csum[:, :]), n)

            with dve.Fori(0, SINKHORN_ITERS - 1) as n:
                columns(n)
                dve.tensor_scalar(Cj[:, :], row_of, cinv[:, 0:1], None, ALU.mult).then_inc(c_ready, 1)
                dve.wait_ge(rowsum_done, n + 1)
                dve.reciprocal(R[:, :], bank[3][:, 0:T]).then_inc(r_ready, 1)
            columns(SINKHORN_ITERS - 1)
            dve.tensor_scalar(scaled[:, :], all_of_row, cinv[:, 0:1], None, ALU.mult).then_inc(scaled_ready, 1)
            dve.wait_ge(rowsumB_done, 1)
            tk = Chain(dve, top_step)
            tk.step(dve.reciprocal(rinv[:, :], bank[3][:, 0:P]))
            tk.step(dve.scalar_tensor_tensor(G[:, :], KB[:, :], cinv[:, 0:1], rinv[:, :], ALU.mult, ALU.mult))
            tk.step(dve.max(top[:, 0, :], G[:, :]))
            tk.step(dve.match_replace(G1[:, :], top[:, 0, :], G[:, :], -1.0))
            tk.step(dve.max(top[:, 1, :], G1[:, :]))
            tk.step(dve.match_replace(G2[:, :], top[:, 1, :], G1[:, :], -1.0))
            dve.tensor_scalar(M_bf[:, :], G2[:, :], 0.0, None, ALU.is_lt).then_inc(m_ready, 1)
            dve.wait_ge(m_ready, 1)
            dve.wait_ge(later_done, 1)
            tk.step(dve.scalar_tensor_tensor(win[:, :], bank[4][:, 0:P], 0.0, M_bf[:, :], ALU.is_equal, ALU.mult))
            tk.step(dve.tensor_tensor_scan(pos[:, :], win[:, :], win[:, :], 0.0, ALU.add, ALU.max))
            dve.tensor_tensor(slot[:, :], pos[:, :], win[:, :], ALU.mult).then_inc(slot_ready, 1)
            dve.tensor_tensor(wgate[:, :], G[:, :], win[:, :], ALU.mult).then_inc(wg_ready, 1)
            dve.wait_ge(slotT_done, 1)
            tk.step(dve.tensor_copy(slotT[:, :], bank[5][:, 0:P]))

            def one_hot(c):
                n = CHUNK * E
                dve.tensor_tensor(onehot[:, c * CHUNK:(c + 1) * CHUNK, :, :].rearrange("p b e j -> p (b e) j"),
                                  slotT[:, c * n:(c + 1) * n].unsqueeze(2).to_broadcast([P, n, CAP]),
                                  slot_no.unsqueeze(1).to_broadcast([P, n, CAP]), ALU.is_equal).then_inc(onehot_ready, 1)

            def copy_onehotT(c):
                dve.wait_ge(ohT_done, c + 1)
                if c >= 2:
                    dve.wait_ge(scat_done, c - 1)
                dve.tensor_copy(onehotT[:, c % 2, :, :], bank[1][:, :].rearrange("p (b s) -> p b s", b=CHUNK))\
                    .then_inc(ohT_copied, 1)

            def add_experts(c):
                dve.wait_ge(scat_done, c + 1)
                if c == 0:
                    dve.wait_ge(h2s_in, 16)
                for b in range(CHUNK):
                    row = c * CHUNK + b
                    ins = dve.scalar_tensor_tensor(res[:, row, :], bank[4][:, b * D:(b + 1) * D], gate_tok[:, row:row + 1],
                                                   h2s[:, row, :], ALU.mult, ALU.add)
                ins.then_inc(res_ready, 1)

            for c in range(NCH):
                one_hot(c)
            dve.wait_ge(slotT_done, 2)
            tk.step(dve.tensor_reduce(gate_tok[:, :], bank[6][:, 0:P].rearrange("p (b e) -> p b e", e=E), AX.X, ALU.add))
            copy_onehotT(0)
            for c in range(NCH):
                if c + 1 < NCH:
                    copy_onehotT(c + 1)
                add_experts(c)


def _constants():
    import numpy as np
    c = np.zeros((P, C_ALL), np.float32)
    p = np.arange(P)
    c[:, C_IDENT:C_IDENT + P] = np.eye(P)
    c[np.arange(T), C_SPREAD + T * (SPT - 1) + np.arange(T)] = 1.0
    c[p, C_GROUP + p // 16] = 1.0
    inv_freq = (1.0 / np.float32(10000.0) ** (np.arange(0, HD, 2, dtype=np.float32) / np.float32(HD))).astype(np.float32)
    angle = np.arange(T, dtype=np.float32)[:, None] * inv_freq[None, :]
    cos = np.cos(angle).astype(np.float32)
    sin = np.sin(angle).astype(np.float32)
    half = HD // 2
    d = p % HD
    c[:, C_COS:C_COS + T] = cos[:, d % half].T
    c[:, C_SIN:C_SIN + T] = (np.where(d < half, -1.0, 1.0)[None, :] * sin[:, d % half]).T
    c[:, C_ALL_OF_ROW:C_ALL_OF_ROW + P] = p[:, None] // E == p[None, :] // E
    c[:, C_ROW_OF:C_ROW_OF + T] = p[:, None] // E == np.arange(T)[None, :]
    c[:, C_LATER:C_LATER + P] = (p[:, None] // E == p[None, :] // E) & (p[:, None] > p[None, :])
    c[:, C_SLOT:C_SLOT + CAP] = np.arange(1, CAP + 1)
    rope = np.zeros((P, T, 32), np.float32)
    for g in range(P // HD):
        for d_in in range(HD):
            for t in range(T):
                row, base = g * HD + d_in, (g % 2) * HD
                rope[row, t, base + d_in] = cos[t, d_in % half]
                if d_in < half:
                    rope[row, t, base + d_in + half] = sin[t, d_in]
                else:
                    rope[row, t, base + d_in - half] = -sin[t, d_in - half]
    return c, rope


def kernel(x, L0_tok_emb_2, L0_tok_emb_3, L0_tok_emb_4, L0_tok_proj_w, L0_tok_proj_b, L0_attn_Wq, L0_attn_bq,
           L0_attn_Wk, L0_attn_bk, L0_attn_Wv, L0_attn_bv, L0_attn_Wo, L0_attn_bo, L0_ffn_gate_weight, L0_ffn_experts):
    import numpy as np
    import concourse.bacc as bacc
    from concourse.bass_utils import run_bass_kernel_spmd

    def swap_halves(b):
        return np.asarray(b).reshape(H, 2, HD // 2)[:, ::-1].reshape(D)

    proj = np.asarray(L0_tok_proj_w).reshape(D, NG, D).transpose(2, 1, 0).reshape(D, NG * D)
    weights = np.concatenate([
        proj, np.asarray(L0_attn_Wv).T, np.asarray(L0_attn_Wo).T, np.asarray(L0_attn_Wq), np.asarray(L0_attn_Wk),
        np.asarray(L0_ffn_gate_weight)[0],
        np.stack([np.asarray(L0_attn_bq), np.asarray(L0_attn_bk), swap_halves(L0_attn_bq), swap_halves(L0_attn_bk)], 1),
    ], axis=1)
    consts, rope = _constants()
    arrays = {
        "x_ids": np.asarray(x), "emb_2": np.asarray(L0_tok_emb_2), "emb_3": np.asarray(L0_tok_emb_3),
        "emb_4": np.asarray(L0_tok_emb_4), "weights": weights,
        "experts": np.asarray(L0_ffn_experts).transpose(1, 0, 2),
        "bias_rows": np.stack([np.asarray(L0_tok_proj_b), np.asarray(L0_attn_bv), np.asarray(L0_attn_bo)]),
        "consts": consts, "rope": rope,
    }
    arrays = {n: np.ascontiguousarray(a) for n, a in arrays.items()}
    nc = bacc.Bacc("TRN2", target_bir_lowering=False, num_devices=1)
    args = [nc.dram_tensor(n, a.shape, mybir.dt.from_np(a.dtype), kind="ExternalInput").ap() for n, a in arrays.items()]
    args.append(nc.dram_tensor("out", (T, S, D), F32, kind="ExternalOutput").ap())
    lm_layer(nc, *args)
    return run_bass_kernel_spmd(nc, [arrays], core_ids=[0]).results[0]["out"]
```

```python
from contextlib import ExitStack

import concourse.bass as bass
from concourse import mybir

F32 = mybir.dt.float32
BF16 = mybir.dt.bfloat16
F16 = mybir.dt.float16
I32 = mybir.dt.int32
U32 = mybir.dt.uint32
ALU = mybir.AluOpType
ACT = mybir.ActivationFunctionType
AX = mybir.AxisListType

P = 128
T, S, D = 16, 128, 128
H = 8
HD = D // H
NG = 3
VOCAB = 25000
E = 8
CAP = S // E
SUPER = 4
TPS = 4
SPT = P // T
SPS = SPT * TPS
SINKHORN_ITERS = 8
LN_EPS = 1e-5
GATE_EPS = 1e-6
ROUND = float(3 * 2 ** 22)
NO_ROW = float(2 ** 20)
UP = 64.0
WINDOW = 4

W_PROJ = 0
W_V = W_PROJ + NG * D
W_O = W_V + D
W_Q = W_O + D
W_K = W_Q + D
W_GATE = W_K + D
W_BIAS = W_GATE + E
W_ALL = W_BIAS + 4

C_IDENT = 0
C_GROUP = C_IDENT + P
C_COS = C_GROUP + 8
C_SIN = C_COS + T
C_ALL_OF_ROW = C_SIN + T
C_ROW_OF = C_ALL_OF_ROW + P
C_LATER = C_ROW_OF + T
C_SLOT = C_LATER + P
C_ALL = C_SLOT + CAP


class Chain:

    def __init__(self, eng, sem, per=0):
        self.eng, self.sem, self.per, self.n = eng, sem, per, 0

    def begin(self):
        self.n = 0

    def step(self, ins, k=0):
        self.n += 1
        ins.then_inc(self.sem, 1)
        self.eng.wait_ge(self.sem, k * self.per + self.n)


def wait_freed(eng, sem, count):
    if not (isinstance(count, int) and count == 0):
        eng.wait_ge(sem, count)


def lm_layer(nc, x_win, emb_2, emb_3, emb_4, weights, experts, bias_rows, consts, rope, pick, edge, out):
    with ExitStack() as ctx:
        def sb(name, shape, dt=F32):
            return ctx.enter_context(nc.sbuf_tensor(name, shape, dt))

        def sem(name):
            return ctx.enter_context(nc.semaphore(name))

        def halves(name, shape):
            return [sb(name + "_hi", shape, F16), sb(name + "_lo", shape, F16)]

        w_sb = sb("w_sb", [P, W_ALL])
        c_sb = sb("c_sb", [P, C_ALL])
        rope_sb = sb("rope_sb", [P, T, 32])
        pick_sb = sb("pick_sb", [P, 2, T * SPS], F16)
        edge_sb = sb("edge_sb", [P, NG, T])
        mean_of = sb("mean_of", [P, P], F16)
        later_bf = sb("later_bf", [P, P], BF16)
        ident_h = sb("ident_h", [P, P], F16)
        exp_sb = sb("exp_sb", [P, E, D])
        exp_h = halves("exp", [P, E, D])
        brow = sb("brow", [P, 3, D])
        brow_h = halves("brow2", [P, 3, D])
        w_h = halves("w", [P, W_Q])
        gw_h = halves("gw", [P, E])
        xi = sb("xi", [P, WINDOW, T], I32)
        xf = sb("xf", [P, WINDOW, T])
        gram = sb("gram", [P, NG, T])
        quot = sb("quot", [P, T])
        idx_all = sb("idx_all", [P, T, NG], U32)
        emb = sb("emb", [P, TPS, NG, D])
        embT = halves("embT", [P, 2, NG * D])
        h = sb("h", [P, TPS, D])
        hb = sb("hb", [P, T, D])
        xn = sb("xn", [P, TPS, D])
        xnT = halves("xnT", [P, SPS, T])
        wq_rot = halves("wq_rot", [P, T, D])
        wk_rot = halves("wk_rot", [P, T, D])
        b_rot = sb("b_rot", [P, 2, T])
        b_rotT = halves("b_rotT", [P, D])
        QT = halves("QT", [P, SPS, T])
        KT = halves("KT", [P, SPS, T])
        V1 = halves("V1", [P, TPS, H, HD + 1])
        Qx = halves("Qx", [P, SPS, H, T])
        smax = sb("smax", [P, SPS])
        prob = sb("prob", [P, SPS, T])
        PT = halves("PT", [P, TPS * H, T])
        Px = halves("Px", [P, TPS * H, SPT, T])
        rden = sb("rden", [P, 2, 2 * H])
        attn = sb("attn", [P, TPS, D])
        attnT = halves("attnT", [P, TPS, D])
        h2 = sb("h2", [P, TPS, D])
        x2 = sb("x2", [P, TPS, D])
        x2T = halves("x2T", [P, T, S])
        stats = [sb(f"stats{n}", [P, TPS, 6]) for n in range(2)]
        mean = [sb(f"mean{n}", [P, TPS]) for n in range(2)]
        mdiff = [sb(f"mdiff{n}", [P, TPS]) for n in range(2)]
        var_eps = [sb(f"var_eps{n}", [P, TPS]) for n in range(2)]
        lnv = [sb(f"lnv{n}", [P, TPS]) for n in range(2)]
        rstd0 = [sb(f"rstd0{n}", [P, TPS]) for n in range(2)]
        nwt = [sb(f"nwt{n}", [P, TPS]) for n in range(2)]
        rstd = [sb(f"rstd{n}", [P, TPS]) for n in range(2)]
        x2s = sb("x2s", [P, T, D])
        x2s_h = halves("x2s2", [P, T, D])
        h2s = sb("h2s", [P, T, D])
        KA = sb("KA", [P, P])
        KB = sb("KB", [P, P])
        R = sb("R", [P, T])
        Cj = sb("Cj", [P, T])
        cinv16 = sb("cinv16", [P, T])
        csum = sb("csum", [P, 1])
        cinv = sb("cinv", [P, 1])
        scaled = sb("scaled", [P, P])
        rinv = sb("rinv", [P, P])
        G = sb("G", [P, P])
        G1 = sb("G1", [P, P])
        G2 = sb("G2", [P, P])
        top = sb("top", [P, 2, 8])
        M_bf = sb("M_bf", [P, P], BF16)
        win = sb("win", [P, P])
        pos = sb("pos", [P, P])
        slot = sb("slot", [P, P])
        wgate = sb("wgate", [P, P])
        slotT = sb("slotT", [P, P])
        gate_tok = sb("gate_tok", [P, T])
        onehot = sb("onehot", [P, T, E, CAP], F16)
        onehotT = sb("onehotT", [P, T, S], F16)
        xg = [sb(f"xg{n}", [P, 2, E, 4, CAP], F16) for n in range(2)]
        yT = sb("yT", [P, 2, 4, E, CAP])
        y = [sb(f"y{n}", [P, 2, 4, D], F16) for n in range(2)]
        res = sb("res", [P, T, D])

        bank = [ctx.enter_context(nc.psum_tensor(f"bank{n}", [P, 512], F32)) for n in range(8)]
        EMBT, HX, QB, KB_, VB, SB, PB = (0, 1), 2, 3, 4, 5, 6, 7

        h2_dram = nc.dram_tensor("h2_scratch", (S * T, D), F32, kind="Internal").ap()
        x2_dram = nc.dram_tensor("x2_scratch", (S * T, D), F32, kind="Internal").ap()

        ident = c_sb[:, C_IDENT:C_IDENT + P]
        group = c_sb[:, C_GROUP:C_GROUP + 8]
        row_of = c_sb[:, C_ROW_OF:C_ROW_OF + T]
        all_of_row = c_sb[:, C_ALL_OF_ROW:C_ALL_OF_ROW + P]
        slot_no = c_sb[:, C_SLOT:C_SLOT + CAP]

        x_in, c_in, w_in, rope_in, exp_in, brow_in, pick_in = (
            sem(n) for n in ("x_in", "c_in", "w_in", "rope_in", "exp_in", "brow_in", "pick_in"))
        ids_step, idx_ready = sem("ids_step"), sem("idx_ready")
        emb_cleared, pick_cleared = sem("emb_cleared"), sem("pick_cleared")
        gathered = [sem(f"gathered{n}") for n in range(TPS)]
        rope_mm, rope_hi, rope_lo, setup_step, setup_done, brotT_done, brotT_hi, brotT_lo = (
            sem(n) for n in ("rope_mm", "rope_hi", "rope_lo", "setup_step", "setup_done", "brotT_done", "brotT_hi",
                             "brotT_lo"))
        embT_done, embT_hi, embT_lo, proj_done = (sem(n) for n in ("embT_done", "embT_hi", "embT_lo", "proj_done"))
        a_step, b_step = sem("a_step"), sem("b_step")
        h_ready, hb_done = sem("h_ready"), sem("hb_done")
        var_ready = [sem("var1_ready"), sem("var2_ready")]
        ln_log = [sem("ln1_log"), sem("ln2_log")]
        rstd0_ready = [sem("rstd1_guess"), sem("rstd2_guess")]
        xn_ready, xnT_done, xnT_hi, xnT_lo = (sem(n) for n in ("xn_ready", "xnT_done", "xnT_hi", "xnT_lo"))
        q_done, k_done, v_done = sem("q_done"), sem("k_done"), sem("v_done")
        q_hi, k_hi, v_hi, q_lo, k_lo, v_lo = (sem(n) for n in ("q_hi", "k_hi", "v_hi", "q_lo", "k_lo", "v_lo"))
        qx_v, qx_a = sem("qx_v"), sem("qx_a")
        scores_done, shifted, probs_ready = sem("scores_done"), sem("shifted"), sem("probs_ready")
        PT_done, PT_hi, PT_lo, px_v, px_a = (sem(n) for n in ("PT_done", "PT_hi", "PT_lo", "px_v", "px_a"))
        pv_done, attn_ready, attnT_done, attnT_hi, attnT_lo = (
            sem(n) for n in ("pv_done", "attn_ready", "attnT_done", "attnT_hi", "attnT_lo"))
        wo_done, h2_ready, x2_ready, x2T_done, x2T_hi, x2T_lo = (
            sem(n) for n in ("wo_done", "h2_ready", "x2_ready", "x2T_done", "x2T_hi", "x2T_lo"))
        h2_stored, x2_stored, h2s_in, x2s_in = (sem(n) for n in ("h2_stored", "x2_stored", "h2s_in", "x2s_in"))
        x2s_hi, x2s_lo, exp_hi, exp_lo = (sem(n) for n in ("x2s_hi", "x2s_lo", "exp_hi", "exp_lo"))
        logits_done, ka_ready, kaT_done, kb_ready = (
            sem(n) for n in ("logits_done", "ka_ready", "kaT_done", "kb_ready"))
        r_ready, colsum_done, c_ready, rowsum_done, sink_step = (
            sem(n) for n in ("r_ready", "colsum_done", "c_ready", "rowsum_done", "sink_step"))
        scaled_ready, rowsumB_done, top_step, m_ready, later_done = (
            sem(n) for n in ("scaled_ready", "rowsumB_done", "top_step", "m_ready", "later_done"))
        slot_ready, wg_ready, slotT_done, onehot_ready = (
            sem(n) for n in ("slot_ready", "wg_ready", "slotT_done", "onehot_ready"))
        xg_done, xg_hi, xg_lo, ohT_done, ohT_copied = (
            sem(n) for n in ("xg_done", "xg_hi", "xg_lo", "ohT_done", "ohT_copied"))
        yT_done, yT_copied, y_done, y_hi, y_lo, scat_done, res_ready = (
            sem(n) for n in ("yT_done", "yT_copied", "y_done", "y_hi", "y_lo", "scat_done", "res_ready"))
        gate_ready, split_done, out_stored = sem("gate_ready"), sem("split_done"), sem("out_stored")

        MASKS_V = 6
        CHUNK = 4
        NCH = T // CHUNK

        block = ctx.enter_context(nc.Block())

        @block.sync
        def _(sp):
            sp.dma_start(xi[:, :, :], x_win).then_inc(x_in, 16)
            sp.dma_start(edge_sb[:, :, :], edge).then_inc(x_in, 16)
            sp.dma_start(c_sb[:, :], consts).then_inc(c_in, 16)
            sp.dma_start(w_sb[:, :], weights).then_inc(w_in, 16)
            sp.dma_start(rope_sb[:, :, :], rope).then_inc(rope_in, 16)
            sp.dma_start(brow[:, :, :], bias_rows.partition_broadcast(P)).then_inc(brow_in, 16)
            sp.wait_ge(pick_cleared, 1)
            sp.dma_start(pick_sb[0:2 * T, :, :], pick.rearrange("p n t s -> p n (t s)")).then_inc(pick_in, 16)
            sp.dma_start(exp_sb[:, :, :], experts).then_inc(exp_in, 16)

            with sp.Fori(0, SUPER) as k:
                rows = bass.ds(k * (TPS * P), TPS * P)
                sp.wait_ge(h2_ready, k + 1)
                sp.dma_start(h2_dram[rows, :].rearrange("(i p) d -> p i d", p=P), h2[:, :, :]).then_inc(h2_stored, 16)
                sp.wait_ge(x2_ready, k + 1)
                sp.dma_start(x2_dram[rows, :].rearrange("(i p) d -> p i d", p=P), x2[:, :, :]).then_inc(x2_stored, 16)
            sp.wait_ge(x2_stored, 16 * SUPER)
            sp.dma_start(x2s[:, :, :], x2_dram.rearrange("(s t) d -> s t d", t=T)).then_inc(x2s_in, 16)
            sp.wait_ge(h2_stored, 16 * SUPER)
            sp.dma_start(h2s[:, :, :], h2_dram.rearrange("(s t) d -> s t d", t=T)).then_inc(h2s_in, 16)
            for c in range(NCH):
                sp.wait_ge(res_ready, c + 1)
                sp.dma_start(out[c * CHUNK:(c + 1) * CHUNK, :, :].rearrange("b s d -> s b d"),
                             res[:, c * CHUNK:(c + 1) * CHUNK, :]).then_inc(out_stored, 16)
            sp.wait_ge(out_stored, 16 * NCH)

        @block.gpsimd
        def _(pool):
            tables = (emb_2, emb_3, emb_4)

            def gather(k):
                for i in range(TPS):
                    if k > 0:
                        pool.wait_ge(embT_done, TPS * (k - 1) + i + 1)
                    tile = k * TPS + i
                    if tile == T - 1:
                        pool.memset(emb[:, i, :, :], 0.0).then_inc(emb_cleared, 1)
                        pool.wait_ge(emb_cleared, 2)
                    for n in range(NG):
                        if tile == 0:
                            pool.wait_ge(idx_ready, n + 1)
                        pool.indirect_dma_start(
                            emb[:, i, n, :], None, tables[n],
                            bass.IndirectOffsetOnAxis(ap=idx_all[:, tile, n:n + 1], axis=0),
                            bounds_check=VOCAB - 1, oob_is_err=False).then_inc(gathered[i], 16)

            def add_bo(k):
                pool.wait_ge(h_ready, k + 1)
                pool.tensor_tensor(hb[:, k * TPS:(k + 1) * TPS, :], h[:, :, :],
                                   brow[:, 2:3, :].to_broadcast([P, TPS, D]), ALU.add).then_inc(hb_done, 1)

            pool.memset(emb[:, 0, :, :], 0.0).then_inc(emb_cleared, 1)
            pool.wait_ge(emb_cleared, 1)
            pool.memset(pick_sb[:, :, :], 0.0).then_inc(pick_cleared, 1)
            gather(0)
            pool.wait_ge(brow_in, 16)
            for k in range(1, SUPER):
                gather(k)
                add_bo(k - 1)
            add_bo(SUPER - 1)
            pool.wait_ge(x2s_hi, 1)
            pool.tensor_tensor(x2s_h[1][:, :, :], x2s[:, :, :], x2s_h[0][:, :, :], ALU.subtract).then_inc(x2s_lo, 1)

        @block.scalar
        def _(act):
            def guess_rstd(n, k):
                act.wait_ge(var_ready[n], k + 1)
                act.activation(lnv[n][:, :], var_eps[n][:, :], ACT.Ln).then_inc(ln_log[n], 1)
                act.wait_ge(ln_log[n], k + 1)
                act.activation(rstd0[n][:, :], lnv[n][:, :], ACT.Exp, scale=-0.5).then_inc(rstd0_ready[n], 1)

            def embed(k):
                for i in range(TPS):
                    act.wait_ge(embT_done, k * TPS + i + 1)
                    if not (isinstance(k, int) and k == 0 and i < 2):
                        act.wait_ge(proj_done, k * TPS + i - 1)
                    act.activation(embT[0][:, i % 2, :], bank[EMBT[i % 2]][:, 0:NG * D], ACT.Copy).then_inc(embT_hi, 1)
                act.wait_ge(proj_done, TPS * (k + 1))
                wait_freed(act, hb_done, k)
                act.activation(h[:, :, :], bank[HX][:, :].rearrange("p (i d) -> p i d", d=D), ACT.Copy,
                               scale=1 / UP).then_inc(h_ready, 1)
                guess_rstd(0, k)

            def copy_xnT(k):
                act.wait_ge(xnT_done, k + 1)
                wait_freed(act, v_done, k)
                act.activation(xnT[0][:, :, :], bank[HX][:, :].rearrange("p (s t) -> p s t", t=T),
                               ACT.Copy).then_inc(xnT_hi, 1)

            def take_qk(k):
                act.wait_ge(q_done, k + 1)
                wait_freed(act, qx_v, k)
                act.activation(QT[0][:, :, :].rearrange("p s t -> p t s"), bank[QB][:, :].rearrange("p (t s) -> p t s", t=T),
                               ACT.Copy).then_inc(q_hi, 1)
                act.wait_ge(k_done, k + 1)
                wait_freed(act, scores_done, k)
                act.activation(KT[0][:, :, :].rearrange("p s t -> p t s"), bank[KB_][:, :].rearrange("p (t s) -> p t s", t=T),
                               ACT.Copy).then_inc(k_hi, 1)
                act.wait_ge(q_lo, k + 1)
                for part in range(2):
                    for g in range(MASKS_V, H):
                        ins = act.activation(Qx[part][:, :, g, :], QT[part][:, :, :], ACT.Copy, scale=group[:, g:g + 1])
                ins.then_inc(qx_a, 1)

            def take_v(k):
                act.wait_ge(v_done, k + 1)
                wait_freed(act, pv_done, k)
                act.activation(V1[0][:, :, :, 0:HD], bank[VB][:, :].rearrange("p (i g d) -> p i g d", i=TPS, d=HD),
                               ACT.Copy).then_inc(v_hi, 1)

            def exps(k):
                act.wait_ge(shifted, k + 1)
                act.activation(prob[:, :, :], prob[:, :, :], ACT.Exp, scale=1 / UP ** 2).then_inc(probs_ready, 1)

            def take_p(k):
                act.wait_ge(PT_done, k + 1)
                wait_freed(act, px_v, k)
                act.activation(PT[0][:, :, :], bank[PB][:, :].rearrange("p (a t) -> p a t", t=T), ACT.Copy).then_inc(PT_hi, 1)
                act.wait_ge(PT_lo, k + 1)
                for part in range(2):
                    for g in range(MASKS_V, SPT):
                        ins = act.activation(Px[part][:, :, g, :], PT[part][:, :, :], ACT.Copy, scale=group[:, g:g + 1])
                ins.then_inc(px_a, 1)

            def copy_attnT(k):
                act.wait_ge(attnT_done, k + 1)
                act.activation(attnT[0][:, :, :], bank[SB][:, :].rearrange("p (i d) -> p i d", d=D),
                               ACT.Copy).then_inc(attnT_hi, 1)

            def copy_x2T(k):
                act.wait_ge(x2T_done, k + 1)
                dst = x2T[0][:, :, k * SPS:(k + 1) * SPS] if isinstance(k, int) else x2T[0][:, :, bass.ds(k * SPS, SPS)]
                act.activation(dst.rearrange("p t s -> p s t"), bank[PB][:, :].rearrange("p (s t) -> p s t", t=T),
                               ACT.Copy).then_inc(x2T_hi, 1)

            act.preload_act_table_set("natural_log_exp_and_others")
            for n, w in enumerate((wq_rot, wk_rot)):
                for j in range(4):
                    act.wait_ge(rope_mm, 4 * n + j + 1)
                    act.activation(w[0][:, :, 32 * j:32 * j + 32], bank[4 + j][:, :].rearrange("p (t c) -> p t c", c=32),
                                   ACT.Copy, scale=UP * (HD ** -0.5 if n == 0 else 1.0)).then_inc(rope_hi, 1)
            act.wait_ge(brotT_done, 1)
            act.activation(b_rotT[0][0:2 * T, :], bank[3][0:2 * T, 0:D], ACT.Copy).then_inc(brotT_hi, 1)
            embed(0)
            copy_xnT(0)
            take_qk(0)
            take_v(0)

            def supertile(k, before, after):
                if after:
                    embed(k + 1)
                exps(k)
                if before:
                    copy_x2T(k - 1)
                if after:
                    copy_xnT(k + 1)
                take_p(k)
                if after:
                    take_qk(k + 1)
                    take_v(k + 1)
                copy_attnT(k)
                guess_rstd(1, k)

            supertile(0, False, True)
            with act.Fori(1, SUPER - 1) as k:
                supertile(k, True, True)
            act.wait_ge(exp_in, 16)
            act.activation(exp_h[0][:, :, :], exp_sb[:, :, :], ACT.Copy, scale=UP).then_inc(exp_hi, 1)
            supertile(SUPER - 1, True, False)
            copy_x2T(SUPER - 1)

            act.wait_ge(x2s_in, 16)
            act.activation(x2s_h[0][:, :, :], x2s[:, :, :], ACT.Copy).then_inc(x2s_hi, 1)
            for step in range(NCH + 2):
                if step < NCH:
                    c = step
                    act.wait_ge(xg_done, c + 1)
                    if c >= 2:
                        act.wait_ge(yT_done, c - 1)
                    act.activation(xg[0][:, c % 2, :, :, :].rearrange("p e b j -> p b e j"),
                                   bank[0][:, :].rearrange("p (b e j) -> p b e j", b=CHUNK, e=E), ACT.Copy).then_inc(xg_hi, 1)
                if 1 <= step <= NCH:
                    c = step - 1
                    act.wait_ge(yT_done, c + 1)
                    act.activation(yT[:, c % 2, :, :, :].rearrange("p b e j -> p e b j"),
                                   bank[3][:, :].rearrange("p (e b j) -> p e b j", b=CHUNK, e=E), ACT.Copy).then_inc(yT_copied, 1)
                if 2 <= step:
                    c = step - 2
                    act.wait_ge(y_done, c + 1)
                    if c >= 2:
                        act.wait_ge(scat_done, c - 1)
                    act.activation(y[0][:, c % 2, :, :], bank[4][:, :].rearrange("p (b d) -> p b d", b=CHUNK),
                                   ACT.Copy).then_inc(y_hi, 1)

        @block.tensor
        def _(pe):
            def product(dst, w, x, start=True, stop=True):
                pe.matmul(dst, w[0], x[0], start=start, stop=False)
                pe.matmul(dst, w[0], x[1], start=False, stop=False)
                return pe.matmul(dst, w[1], x[0], start=False, stop=stop)

            def bias(dst, n):
                for part in range(2):
                    pe.matmul(dst, mean_of[:, :], brow_h[part][:, n:n + 1, :].to_broadcast([P, TPS, D]),
                              start=(part == 0), stop=False)

            pe.wait_ge(w_in, 16)
            pe.wait_ge(rope_in, 16)
            for n, w0 in enumerate((W_Q, W_K)):
                for j in range(4):
                    if n == 1:
                        pe.wait_ge(rope_lo, j + 1)
                    pe.matmul(bank[4 + j][:, :], w_sb[32 * j:32 * j + 32, w0:w0 + D],
                              rope_sb[32 * j:32 * j + 32, :, :], start=True, stop=True).then_inc(rope_mm, 1)
            pe.wait_ge(setup_done, 1)
            pe.transpose(bank[3][0:2 * T, 0:D], b_rot[:, :, :].rearrange("p n t -> p (n t)"), ident).then_inc(brotT_done, 1)

            def embed(k):
                def turn(i):
                    pe.wait_ge(gathered[i], (k + 1) * (16 * NG))
                    if i < 2:
                        if not isinstance(k, int) or k > 1:
                            pe.wait_ge(attn_ready, k - 1)
                    else:
                        pe.wait_ge(embT_lo, k * TPS + i - 1)
                    for n in range(NG):
                        ins = pe.transpose(bank[EMBT[i % 2]][:, n * D:(n + 1) * D], emb[:, i, n, :], ident)
                    ins.then_inc(embT_done, 1)

                def project(i):
                    pe.wait_ge(embT_hi, k * TPS + i + 1)
                    pe.wait_ge(embT_lo, k * TPS + i + 1)
                    for n in range(NG):
                        ins = product(bank[HX][:, i * D:(i + 1) * D],
                                      [embT[part][:, i % 2, n * D:(n + 1) * D] for part in range(2)],
                                      [w_h[part][:, W_PROJ + n * D:W_PROJ + (n + 1) * D] for part in range(2)],
                                      start=False, stop=(i == TPS - 1 and n == NG - 1))
                    ins.then_inc(proj_done, 1)

                turn(0)
                wait_freed(pe, xnT_lo, k)
                bias(bank[HX][:, :], 0)
                for i in range(1, TPS):
                    turn(i)
                    project(i - 1)
                project(TPS - 1)

            def transpose_xn(k):
                pe.wait_ge(xn_ready, k + 1)
                for i in range(TPS):
                    ins = pe.transpose(bank[HX][:, i * D:(i + 1) * D], xn[:, i, :], ident)
                ins.then_inc(xnT_done, 1)

            def qkv(k):
                pe.wait_ge(xnT_hi, k + 1)
                pe.wait_ge(xnT_lo, k + 1)
                wait_freed(pe, v_lo, k)
                for n, (b, w, done) in enumerate(((QB, wq_rot, q_done), (KB_, wk_rot, k_done))):
                    for part in range(2):
                        pe.matmul(bank[b][:, :], b_rotT[part][:, :], pick_sb[:, n, :], start=(part == 0), stop=False)
                    for t in range(T):
                        ins = product(bank[b][:, t * SPS:(t + 1) * SPS], [w[part][:, t, :] for part in range(2)],
                                      [xnT[part][:, :, t] for part in range(2)], start=False, stop=(t == T - 1))
                    ins.then_inc(done, 1)
                bias(bank[VB][:, :], 1)
                for i in range(TPS):
                    ins = product(bank[VB][:, i * D:(i + 1) * D],
                                  [xnT[part][:, i * SPT:(i + 1) * SPT, :].rearrange("p s t -> p (s t)") for part in range(2)],
                                  [w_h[part][:, W_V:W_V + D] for part in range(2)], start=False, stop=(i == TPS - 1))
                ins.then_inc(v_done, 1)

            def scores(k):
                pe.wait_ge(k_lo, k + 1)
                pe.wait_ge(qx_v, k + 1)
                pe.wait_ge(qx_a, k + 1)
                wait_freed(pe, attnT_lo, k)
                for s in range(SPS):
                    ins = product(bank[SB][:, s * T:(s + 1) * T],
                                  [Qx[part][:, s, :, :].rearrange("p g t -> p (g t)") for part in range(2)],
                                  [KT[part][:, s, :] for part in range(2)])
                ins.then_inc(scores_done, 1)

            def transpose_x2(k):
                pe.wait_ge(x2_ready, k + 1)
                for i in range(TPS):
                    ins = pe.transpose(bank[PB][:, i * D:(i + 1) * D], x2[:, i, :], ident)
                ins.then_inc(x2T_done, 1)

            def transpose_prob(k):
                pe.wait_ge(probs_ready, k + 1)
                wait_freed(pe, x2T_lo, k)
                for i in range(TPS):
                    ins = pe.transpose(bank[PB][:, i * P:(i + 1) * P],
                                       prob[:, i * SPT:(i + 1) * SPT, :].rearrange("p s t -> p (s t)"), ident)
                ins.then_inc(PT_done, 1)

            def weigh_v(k):
                pe.wait_ge(px_v, k + 1)
                pe.wait_ge(px_a, k + 1)
                pe.wait_ge(v_lo, k + 1)
                for i in range(TPS):
                    for g in range(H):
                        at = ((i % 2) * H + g) * (HD + 1)
                        ins = product(bank[EMBT[i // 2]][:, at:at + HD + 1],
                                      [Px[part][:, i * H + g, :, :].rearrange("p s t -> p (s t)") for part in range(2)],
                                      [V1[part][:, i, g, :] for part in range(2)])
                ins.then_inc(pv_done, 1)

            def project_out(k):
                pe.wait_ge(attn_ready, k + 1)
                for i in range(TPS):
                    ins = pe.transpose(bank[SB][:, i * D:(i + 1) * D], attn[:, i, :], ident)
                ins.then_inc(attnT_done, 1)
                pe.wait_ge(attnT_lo, k + 1)
                for i in range(TPS):
                    ins = product(bank[PB][:, i * D:(i + 1) * D], [attnT[part][:, i, :] for part in range(2)],
                                  [w_h[part][:, W_O:W_O + D] for part in range(2)])
                ins.then_inc(wo_done, 1)

            pe.wait_ge(split_done, 1)
            embed(0)
            transpose_xn(0)
            pe.wait_ge(rope_lo, 8)
            pe.wait_ge(brotT_lo, 1)
            pe.wait_ge(pick_in, 16)
            qkv(0)

            def supertile(k, before, after):
                if after:
                    embed(k + 1)
                scores(k)
                if before:
                    transpose_x2(k - 1)
                if after:
                    transpose_xn(k + 1)
                transpose_prob(k)
                if after:
                    qkv(k + 1)
                weigh_v(k)
                project_out(k)

            supertile(0, False, True)
            with pe.Fori(1, SUPER - 1) as k:
                supertile(k, True, True)
            supertile(SUPER - 1, True, False)
            transpose_x2(SUPER - 1)

            pe.wait_ge(x2T_hi, SUPER)
            pe.wait_ge(x2T_lo, SUPER)
            for b in range(T):
                ins = product(bank[0][:, b * E:(b + 1) * E], [x2T[part][:, b, :] for part in range(2)],
                              [gw_h[part][:, :] for part in range(2)])
            ins.then_inc(logits_done, 1)
            pe.wait_ge(ka_ready, 1)
            pe.transpose(bank[1][:, 0:P], KA[:, :], ident).then_inc(kaT_done, 1)
            with pe.Fori(0, SINKHORN_ITERS - 1) as n:
                pe.wait_ge(r_ready, n + 1)
                pe.matmul(bank[2][:, 0:T], KA[:, :], R[:, :], start=True, stop=True).then_inc(colsum_done, 1)
                pe.wait_ge(c_ready, n + 1)
                pe.matmul(bank[3][:, 0:T], KB[:, :], Cj[:, :], start=True, stop=True).then_inc(rowsum_done, 1)
            pe.wait_ge(r_ready, SINKHORN_ITERS)
            pe.matmul(bank[2][:, 0:T], KA[:, :], R[:, :], start=True, stop=True).then_inc(colsum_done, 1)
            pe.wait_ge(scaled_ready, 1)
            pe.matmul(bank[3][:, 0:P], scaled[:, :], KB[:, :], start=True, stop=True).then_inc(rowsumB_done, 1)
            pe.wait_ge(m_ready, 1)
            pe.matmul(bank[4][:, 0:P], later_bf[:, :], M_bf[:, :], start=True, stop=True).then_inc(later_done, 1)
            pe.wait_ge(slot_ready, 1)
            pe.transpose(bank[5][:, 0:P], slot[:, :], ident).then_inc(slotT_done, 1)
            pe.wait_ge(wg_ready, 1)
            pe.transpose(bank[6][:, 0:P], wgate[:, :], ident).then_inc(slotT_done, 1)

            pe.wait_ge(x2s_hi, 1)
            pe.wait_ge(x2s_lo, 1)
            pe.wait_ge(exp_hi, 1)
            pe.wait_ge(exp_lo, 1)
            ohT_bank = [bank[6 + n][:, 0:256].bitcast(F16) for n in range(2)]

            def gather(c):
                pe.wait_ge(onehot_ready, c + 1)
                if c >= 1:
                    pe.wait_ge(xg_hi, c)
                    pe.wait_ge(xg_lo, c)
                for part in range(2):
                    for b in range(CHUNK):
                        ins = pe.matmul(bank[part][:, b * P:(b + 1) * P], x2s_h[part][:, c * CHUNK + b, :],
                                        onehot[:, c * CHUNK + b, :, :], start=True, stop=True)
                ins.then_inc(xg_done, 1)
                if c == 0:
                    pe.wait_ge(gate_ready, 1)
                if c >= 2:
                    pe.wait_ge(ohT_copied, c - 1)
                for b in range(CHUNK):
                    ins = pe.transpose(ohT_bank[c % 2][:, b * P:(b + 1) * P],
                                       onehot[:, c * CHUNK + b, :, :].rearrange("p e j -> p (e j)"), ident_h[:, :])
                ins.then_inc(ohT_done, 1)

            def apply_experts(c):
                pe.wait_ge(xg_hi, c + 1)
                pe.wait_ge(xg_lo, c + 1)
                if c >= 1:
                    pe.wait_ge(yT_copied, c)
                w = CHUNK * CAP
                for e in range(E):
                    ins = product(bank[3][:, e * w:(e + 1) * w], [exp_h[part][:, e, :] for part in range(2)],
                                  [xg[part][:, c % 2, e, :, :] for part in range(2)])
                ins.then_inc(yT_done, 1)

            def turn_y(c):
                pe.wait_ge(yT_copied, c + 1)
                if c >= 1:
                    pe.wait_ge(y_lo, c)
                for b in range(CHUNK):
                    ins = pe.transpose(bank[4][:, b * P:(b + 1) * P],
                                       yT[:, c % 2, b, :, :].rearrange("p e j -> p (e j)"), ident)
                ins.then_inc(y_done, 1)

            def scatter(c):
                pe.wait_ge(y_hi, c + 1)
                pe.wait_ge(y_lo, c + 1)
                pe.wait_ge(ohT_copied, c + 1)
                if c >= 1:
                    pe.wait_ge(res_ready, c)
                for b in range(CHUNK):
                    for part in range(2):
                        ins = pe.matmul(bank[5][:, b * D:(b + 1) * D], onehotT[:, c * CHUNK + b, :],
                                        y[part][:, c % 2, b, :], start=(part == 0), stop=(part == 1))
                ins.then_inc(scat_done, 1)

            for step in range(NCH + 3):
                if step < NCH:
                    gather(step)
                if 1 <= step <= NCH:
                    apply_experts(step - 1)
                if 3 <= step:
                    scatter(step - 3)
                if 2 <= step <= NCH + 1:
                    turn_y(step - 2)

        @block.vector
        def _(dve):
            ids = Chain(dve, ids_step)

            def mod_vocab(v):
                ids.step(dve.tensor_scalar(quot[:, :], v, 1.0 / VOCAB, 0.5 / VOCAB - 0.5, ALU.mult, ALU.add))
                ids.step(dve.tensor_scalar(quot[:, :], quot[:, :], ROUND, -ROUND, ALU.add, ALU.add))
                ids.step(dve.scalar_tensor_tensor(v, quot[:, :], -float(VOCAB), v, ALU.mult, ALU.add))

            def emit(n):
                dve.tensor_tensor(idx_all[:, :, n], gram[:, n, :], edge_sb[:, n, :], ALU.add).then_inc(idx_ready, 1)

            def shift_in(dst, prev, byte):
                ids.step(dve.scalar_tensor_tensor(dst, prev, 64.0, byte, ALU.mult, ALU.add))

            dve.wait_ge(x_in, 32)
            ids.step(dve.tensor_copy(xf[:, :, :], xi[:, :, :]))
            shift_in(gram[:, 0, :], xf[:, 1, :], xf[:, 2, :])
            emit(0)
            shift_in(gram[:, 1, :], gram[:, 0, :], xf[:, 3, :])
            mod_vocab(gram[:, 1, :])
            emit(1)
            shift_in(gram[:, 2, :], xf[:, 0, :], xf[:, 1, :])
            shift_in(gram[:, 2, :], gram[:, 2, :], xf[:, 2, :])
            mod_vocab(gram[:, 2, :])
            shift_in(gram[:, 2, :], gram[:, 2, :], xf[:, 3, :])
            mod_vocab(gram[:, 2, :])
            emit(2)

            setup = Chain(dve, setup_step)
            setup.step(dve.memset(mean_of[:, :], 1.0 / P))
            for part, value in ((0, 1.0), (1, 0.0)):
                setup.step(dve.memset(V1[part][:, :, :, HD:HD + 1], value))
                setup.step(dve.memset(b_rotT[part][:, :], 0.0))
            dve.wait_ge(c_in, 16)
            dve.wait_ge(w_in, 16)
            for n, scale in ((0, UP * HD ** -0.5), (1, UP)):
                setup.step(dve.tensor_scalar(b_rot[:, n, :], c_sb[:, C_COS:C_COS + T],
                                             w_sb[:, W_BIAS + n:W_BIAS + n + 1], scale, ALU.mult, ALU.mult))
                setup.step(dve.tensor_scalar(rden[:, n, :], c_sb[:, C_SIN:C_SIN + T],
                                             w_sb[:, W_BIAS + 2 + n:W_BIAS + 3 + n], scale, ALU.mult, ALU.mult))
                setup.step(dve.tensor_tensor(b_rot[:, n, :], b_rot[:, n, :], rden[:, n, :], ALU.add))
            dve.memset(R[:, :], 1.0).then_inc(setup_done, 1)
            for n, (w, scale) in enumerate(((wq_rot, UP * HD ** -0.5), (wk_rot, UP))):
                for j in range(4):
                    dve.wait_ge(rope_hi, 4 * n + j + 1)
                    dve.scalar_tensor_tensor(w[1][:, :, 32 * j:32 * j + 32],
                                             bank[4 + j][:, :].rearrange("p (t c) -> p t c", c=32), scale,
                                             w[0][:, :, 32 * j:32 * j + 32], ALU.mult, ALU.subtract).then_inc(rope_lo, 1)
            dve.wait_ge(brotT_hi, 1)
            dve.tensor_tensor(b_rotT[1][0:2 * T, :], bank[3][0:2 * T, 0:D], b_rotT[0][0:2 * T, :],
                              ALU.subtract).then_inc(brotT_lo, 1)
            dve.wait_ge(brow_in, 16)

            def split(dst, src, scale):
                setup.step(dve.tensor_scalar(dst[0], src, scale, None, ALU.mult))
                setup.step(dve.scalar_tensor_tensor(dst[1], src, scale, dst[0], ALU.mult, ALU.subtract))

            split([p[:, :] for p in w_h], w_sb[:, 0:W_Q], UP)
            split([p[:, :, :] for p in brow_h], brow[:, :, :], UP)
            split([p[:, :] for p in gw_h], w_sb[:, W_GATE:W_GATE + E], UP)
            setup.step(dve.tensor_copy(later_bf[:, :], c_sb[:, C_LATER:C_LATER + P]))
            dve.tensor_copy(ident_h[:, :], ident).then_inc(split_done, 1)

            def layernorm(n, k, chain, src, dst, ready):
                for i in range(TPS):
                    ins = dve.bn_stats(stats[n][:, i, :], src[:, i, :])
                chain.step(ins, k)
                even, odd = stats[n][:, :, 1], stats[n][:, :, 4]
                dve.tensor_tensor(mean[n][:, :], even, odd, ALU.add)
                dve.tensor_tensor(mdiff[n][:, :], even, odd, ALU.subtract)
                chain.step(dve.tensor_tensor(var_eps[n][:, :], stats[n][:, :, 2], stats[n][:, :, 5], ALU.add), k)
                dve.tensor_scalar(mean[n][:, :], mean[n][:, :], 0.5, None, ALU.mult)
                dve.tensor_scalar(var_eps[n][:, :], var_eps[n][:, :], 1.0 / D, LN_EPS, ALU.mult, ALU.add)
                chain.step(dve.scalar_tensor_tensor(mdiff[n][:, :], mdiff[n][:, :], 0.25, mdiff[n][:, :],
                                                    ALU.mult, ALU.mult), k)
                dve.tensor_tensor(var_eps[n][:, :], var_eps[n][:, :], mdiff[n][:, :], ALU.add).then_inc(var_ready[n], 1)
                dve.wait_ge(rstd0_ready[n], k + 1)
                chain.step(dve.tensor_tensor(nwt[n][:, :], rstd0[n][:, :], rstd0[n][:, :], ALU.mult), k)
                chain.step(dve.tensor_tensor(nwt[n][:, :], nwt[n][:, :], var_eps[n][:, :], ALU.mult), k)
                chain.step(dve.tensor_scalar(nwt[n][:, :], nwt[n][:, :], -0.5, 1.5, ALU.mult, ALU.add), k)
                chain.step(dve.tensor_tensor(rstd[n][:, :], nwt[n][:, :], rstd0[n][:, :], ALU.mult), k)
                for i in range(TPS):
                    ins = dve.tensor_scalar(dst[:, i, :], src[:, i, :], mean[n][:, i:i + 1], rstd[n][:, i:i + 1],
                                            ALU.subtract, ALU.mult)
                ins.then_inc(ready, 1)

            ach = Chain(dve, a_step, per=7)
            bch = Chain(dve, b_step, per=9)

            def low(dst, src, hi, hi_ready, count, ready):
                dve.wait_ge(hi_ready, count)
                dve.tensor_tensor(dst, src, hi, ALU.subtract).then_inc(ready, 1)

            def embed(k):
                for i in range(TPS):
                    low(embT[1][:, i % 2, :], bank[EMBT[i % 2]][:, 0:NG * D], embT[0][:, i % 2, :], embT_hi,
                        k * TPS + i + 1, embT_lo)
                dve.wait_ge(h_ready, k + 1)
                ach.begin()
                layernorm(0, k, ach, h, xn, xn_ready)
                assert ach.n == ach.per

            def take_xnT(k):
                low(xnT[1][:, :, :], bank[HX][:, :].rearrange("p (s t) -> p s t", t=T), xnT[0][:, :, :], xnT_hi, k + 1, xnT_lo)

            def take_qk(k):
                wait_freed(dve, qx_a, k)
                low(QT[1][:, :, :].rearrange("p s t -> p t s"), bank[QB][:, :].rearrange("p (t s) -> p t s", t=T),
                    QT[0][:, :, :].rearrange("p s t -> p t s"), q_hi, k + 1, q_lo)
                wait_freed(dve, scores_done, k)
                for g in range(MASKS_V):
                    dve.tensor_scalar(Qx[0][:, :, g, :], QT[0][:, :, :], group[:, g:g + 1], None, ALU.mult)
                dve.wait_ge(q_lo, k + 1)
                for g in range(MASKS_V):
                    ins = dve.tensor_scalar(Qx[1][:, :, g, :], QT[1][:, :, :], group[:, g:g + 1], None, ALU.mult)
                ins.then_inc(qx_v, 1)
                low(KT[1][:, :, :].rearrange("p s t -> p t s"), bank[KB_][:, :].rearrange("p (t s) -> p t s", t=T),
                    KT[0][:, :, :].rearrange("p s t -> p t s"), k_hi, k + 1, k_lo)

            def take_v(k):
                low(V1[1][:, :, :, 0:HD], bank[VB][:, :].rearrange("p (i g d) -> p i g d", i=TPS, d=HD),
                    V1[0][:, :, :, 0:HD], v_hi, k + 1, v_lo)

            def shift(k):
                dve.wait_ge(scores_done, k + 1)
                sc = bank[SB][:, :].rearrange("p (s t) -> p s t", t=T)
                bch.step(dve.tensor_reduce(smax[:, :], sc, AX.X, ALU.max), k)
                dve.tensor_tensor(prob[:, :, :], sc, smax[:, :].unsqueeze(2).to_broadcast([P, SPS, T]),
                                  ALU.subtract).then_inc(shifted, 1)

            def take_p(k):
                wait_freed(dve, px_a, k)
                low(PT[1][:, :, :], bank[PB][:, :].rearrange("p (a t) -> p a t", t=T), PT[0][:, :, :], PT_hi, k + 1, PT_lo)
                for g in range(MASKS_V):
                    dve.tensor_scalar(Px[0][:, :, g, :], PT[0][:, :, :], group[:, g:g + 1], None, ALU.mult)
                dve.wait_ge(PT_lo, k + 1)
                for g in range(MASKS_V):
                    ins = dve.tensor_scalar(Px[1][:, :, g, :], PT[1][:, :, :], group[:, g:g + 1], None, ALU.mult)
                ins.then_inc(px_v, 1)

            def normalise(k):
                dve.wait_ge(pv_done, k + 1)
                o = [bank[EMBT[n]][:, 0:2 * H * (HD + 1)].rearrange("p (a d) -> p a d", d=HD + 1) for n in range(2)]
                for n in range(2):
                    ins = dve.reciprocal(rden[:, n, :], o[n][:, :, HD])
                bch.step(ins, k)
                for n in range(2):
                    ins = dve.tensor_tensor(attn[:, 2 * n:2 * n + 2, :].rearrange("p i (g d) -> p (i g) d", d=HD),
                                            o[n][:, :, 0:HD], rden[:, n, :].unsqueeze(2).to_broadcast([P, 2 * H, HD]),
                                            ALU.mult)
                ins.then_inc(attn_ready, 1)

            def residual(k):
                low(attnT[1][:, :, :], bank[SB][:, :].rearrange("p (i d) -> p i d", d=D), attnT[0][:, :, :],
                    attnT_hi, k + 1, attnT_lo)
                dve.wait_ge(wo_done, k + 1)
                dve.wait_ge(hb_done, k + 1)
                wait_freed(dve, h2_stored, k * 16)
                wait_freed(dve, x2_stored, k * 16)
                src = hb[:, k * TPS:(k + 1) * TPS, :] if isinstance(k, int) else hb[:, bass.ds(k * TPS, TPS), :]
                dve.scalar_tensor_tensor(h2[:, :, :], bank[PB][:, :].rearrange("p (i d) -> p i d", d=D), 1 / UP ** 2, src,
                                         ALU.mult, ALU.add).then_inc(h2_ready, 1)
                dve.wait_ge(h2_ready, k + 1)
                layernorm(1, k, bch, h2, x2, x2_ready)

            def take_x2T(k):
                cols = slice(k * SPS, (k + 1) * SPS) if isinstance(k, int) else bass.ds(k * SPS, SPS)
                low(x2T[1][:, :, cols].rearrange("p t s -> p s t"), bank[PB][:, :].rearrange("p (s t) -> p s t", t=T),
                    x2T[0][:, :, cols].rearrange("p t s -> p s t"), x2T_hi, k + 1, x2T_lo)

            embed(0)
            take_xnT(0)
            take_qk(0)
            take_v(0)

            def supertile(k, before, after):
                bch.begin()
                if after:
                    embed(k + 1)
                shift(k)
                if before:
                    take_x2T(k - 1)
                if after:
                    take_xnT(k + 1)
                take_p(k)
                if after:
                    take_qk(k + 1)
                normalise(k)
                if after:
                    take_v(k + 1)
                residual(k)
                assert bch.n == bch.per

            supertile(0, False, True)
            with dve.Fori(1, SUPER - 1) as k:
                supertile(k, True, True)
            dve.wait_ge(exp_hi, 1)
            dve.scalar_tensor_tensor(exp_h[1][:, :, :].rearrange("p e d -> p (e d)"), exp_sb[:, :, :].rearrange("p e d -> p (e d)"),
                                     UP, exp_h[0][:, :, :].rearrange("p e d -> p (e d)"), ALU.mult,
                                     ALU.subtract).then_inc(exp_lo, 1)
            supertile(SUPER - 1, True, False)
            take_x2T(SUPER - 1)

            sink = Chain(dve, sink_step, per=1)
            dve.wait_ge(logits_done, 1)
            dve.tensor_scalar(KA[:, :], bank[0][:, 0:P], 1 / UP, GATE_EPS, ALU.mult, ALU.max).then_inc(ka_ready, 1)
            dve.wait_ge(ka_ready, 1)
            dve.memset(R[:, :], 1.0).then_inc(r_ready, 1)
            dve.wait_ge(kaT_done, 1)
            dve.tensor_copy(KB[:, :], bank[1][:, 0:P]).then_inc(kb_ready, 1)
            with dve.Fori(0, SINKHORN_ITERS - 1) as n:
                sink.begin()
                dve.wait_ge(colsum_done, n + 1)
                sink.step(dve.reciprocal(cinv16[:, :], bank[2][:, 0:T]), n)
                dve.tensor_tensor(Cj[:, :], cinv16[:, :], row_of, ALU.mult).then_inc(c_ready, 1)
                dve.wait_ge(rowsum_done, n + 1)
                dve.reciprocal(R[:, :], bank[3][:, 0:T]).then_inc(r_ready, 1)
            tk = Chain(dve, top_step)
            dve.wait_ge(colsum_done, SINKHORN_ITERS)
            tk.step(dve.scalar_tensor_tensor(Cj[:, :], bank[2][:, 0:T], 1.0, row_of, ALU.mult, ALU.mult,
                                             accum_out=csum[:, :]))
            tk.step(dve.reciprocal(cinv[:, :], csum[:, :]))
            dve.tensor_scalar(scaled[:, :], all_of_row, cinv[:, 0:1], None, ALU.mult).then_inc(scaled_ready, 1)
            dve.wait_ge(rowsumB_done, 1)
            tk.step(dve.reciprocal(rinv[:, :], bank[3][:, 0:P]))
            tk.step(dve.scalar_tensor_tensor(G[:, :], KB[:, :], cinv[:, 0:1], rinv[:, :], ALU.mult, ALU.mult))
            tk.step(dve.max(top[:, 0, :], G[:, :]))
            tk.step(dve.match_replace(G1[:, :], top[:, 0, :], G[:, :], -1.0))
            tk.step(dve.max(top[:, 1, :], G1[:, :]))
            tk.step(dve.match_replace(G2[:, :], top[:, 1, :], G1[:, :], -1.0))
            dve.tensor_scalar(M_bf[:, :], G2[:, :], 0.0, None, ALU.is_lt).then_inc(m_ready, 1)
            dve.wait_ge(m_ready, 1)
            dve.wait_ge(later_done, 1)
            tk.step(dve.scalar_tensor_tensor(win[:, :], bank[4][:, 0:P], 0.0, M_bf[:, :], ALU.is_equal, ALU.mult))
            tk.step(dve.tensor_tensor_scan(pos[:, :], win[:, :], win[:, :], 0.0, ALU.add, ALU.max))
            dve.tensor_tensor(slot[:, :], pos[:, :], win[:, :], ALU.mult).then_inc(slot_ready, 1)
            dve.scalar_tensor_tensor(wgate[:, :], G[:, :], 1 / UP, win[:, :], ALU.mult, ALU.mult).then_inc(wg_ready, 1)
            dve.wait_ge(slotT_done, 1)
            tk.step(dve.tensor_copy(slotT[:, :], bank[5][:, 0:P]))

            def one_hot(c):
                n = CHUNK * E
                dve.tensor_tensor(onehot[:, c * CHUNK:(c + 1) * CHUNK, :, :].rearrange("p b e j -> p (b e) j"),
                                  slotT[:, c * n:(c + 1) * n].unsqueeze(2).to_broadcast([P, n, CAP]),
                                  slot_no.unsqueeze(1).to_broadcast([P, n, CAP]), ALU.is_equal).then_inc(onehot_ready, 1)

            one_hot(0)
            dve.wait_ge(slotT_done, 2)
            dve.tensor_reduce(gate_tok[:, :], bank[6][:, 0:P].rearrange("p (b e) -> p b e", e=E), AX.X,
                              ALU.add).then_inc(gate_ready, 1)
            for step in range(NCH + 3):
                if step + 1 < NCH:
                    one_hot(step + 1)
                if step < NCH:
                    c = step
                    dve.wait_ge(xg_done, c + 1)
                    if c >= 2:
                        dve.wait_ge(yT_done, c - 1)
                    dve.tensor_copy(xg[1][:, c % 2, :, :, :].rearrange("p e b j -> p b e j"),
                                    bank[1][:, :].rearrange("p (b e j) -> p b e j", b=CHUNK, e=E)).then_inc(xg_lo, 1)
                    dve.wait_ge(ohT_done, c + 1)
                    dve.tensor_copy(onehotT[:, c * CHUNK:(c + 1) * CHUNK, :],
                                    bank[6 + c % 2][:, 0:256].bitcast(F16).rearrange("p (b s) -> p b s", b=CHUNK))\
                        .then_inc(ohT_copied, 1)
                if 2 <= step <= NCH + 1:
                    c = step - 2
                    low(y[1][:, c % 2, :, :], bank[4][:, :].rearrange("p (b d) -> p b d", b=CHUNK),
                        y[0][:, c % 2, :, :], y_hi, c + 1, y_lo)
                if 3 <= step:
                    c = step - 3
                    dve.wait_ge(scat_done, c + 1)
                    if c == 0:
                        dve.wait_ge(gate_ready, 1)
                        dve.wait_ge(h2s_in, 16)
                    for b in range(CHUNK):
                        row = c * CHUNK + b
                        ins = dve.scalar_tensor_tensor(res[:, row, :], bank[5][:, b * D:(b + 1) * D],
                                                       gate_tok[:, row:row + 1], h2s[:, row, :], ALU.mult, ALU.add)
                    ins.then_inc(res_ready, 1)


def _constants():
    import numpy as np
    c = np.zeros((P, C_ALL), np.float32)
    p = np.arange(P)
    c[:, C_IDENT:C_IDENT + P] = np.eye(P)
    c[p, C_GROUP + p // 16] = 1.0
    inv_freq = (1.0 / np.float32(10000.0) ** (np.arange(0, HD, 2, dtype=np.float32) / np.float32(HD))).astype(np.float32)
    angle = np.arange(T, dtype=np.float32)[:, None] * inv_freq[None, :]
    cos = np.cos(angle).astype(np.float32)
    sin = np.sin(angle).astype(np.float32)
    half = HD // 2
    d = p % HD
    c[:, C_COS:C_COS + T] = cos[:, d % half].T
    c[:, C_SIN:C_SIN + T] = (np.where(d < half, -1.0, 1.0)[None, :] * sin[:, d % half]).T
    c[:, C_ALL_OF_ROW:C_ALL_OF_ROW + P] = p[:, None] // E == p[None, :] // E
    c[:, C_ROW_OF:C_ROW_OF + T] = p[:, None] // E == np.arange(T)[None, :]
    c[:, C_LATER:C_LATER + P] = (p[:, None] // E == p[None, :] // E) & (p[:, None] > p[None, :])
    c[:, C_SLOT:C_SLOT + CAP] = np.arange(1, CAP + 1)
    rope = np.zeros((P, T, 32), np.float32)
    for g in range(P // HD):
        for d_in in range(HD):
            for t in range(T):
                row, base = g * HD + d_in, (g % 2) * HD
                rope[row, t, base + d_in] = cos[t, d_in % half]
                if d_in < half:
                    rope[row, t, base + d_in + half] = sin[t, d_in]
                else:
                    rope[row, t, base + d_in - half] = -sin[t, d_in - half]
    pick = np.zeros((2 * T, 2, T, SPS), np.float16)
    for n in range(2):
        for t in range(T):
            pick[n * T + t, n, t, :] = 1.0
    edge = np.zeros((P, NG, T), np.float32)
    for n in range(NG):
        for s in range(S):
            start = s - (n + 2) // 2
            if start < 0 or start + n + 2 > S:
                edge[(s % SPT) * T:(s % SPT + 1) * T, n, s // SPT] = NO_ROW
    return c, rope, pick, edge


def kernel(x, L0_tok_emb_2, L0_tok_emb_3, L0_tok_emb_4, L0_tok_proj_w, L0_tok_proj_b, L0_attn_Wq, L0_attn_bq,
           L0_attn_Wk, L0_attn_bk, L0_attn_Wv, L0_attn_bv, L0_attn_Wo, L0_attn_bo, L0_ffn_gate_weight, L0_ffn_experts):
    import numpy as np
    import concourse.bacc as bacc
    from concourse.bass_utils import run_bass_kernel_spmd

    def swap_halves(b):
        return np.asarray(b).reshape(H, 2, HD // 2)[:, ::-1].reshape(D)

    proj = np.asarray(L0_tok_proj_w).reshape(D, NG, D).transpose(2, 1, 0).reshape(D, NG * D)
    weights = np.concatenate([
        proj, np.asarray(L0_attn_Wv).T, np.asarray(L0_attn_Wo).T, np.asarray(L0_attn_Wq), np.asarray(L0_attn_Wk),
        np.asarray(L0_ffn_gate_weight)[0],
        np.stack([np.asarray(L0_attn_bq), np.asarray(L0_attn_bk), swap_halves(L0_attn_bq), swap_halves(L0_attn_bk)], 1),
    ], axis=1)
    consts, rope, pick, edge = _constants()
    padded = np.pad(np.asarray(x), ((0, 0), (2, 1)))
    x_win = np.stack([padded[:, j:j + S].reshape(T, T, SPT).transpose(2, 0, 1).reshape(P, T) for j in range(WINDOW)], 1)
    arrays = {
        "x_win": x_win, "emb_2": np.asarray(L0_tok_emb_2), "emb_3": np.asarray(L0_tok_emb_3),
        "emb_4": np.asarray(L0_tok_emb_4), "weights": weights,
        "experts": np.asarray(L0_ffn_experts).transpose(1, 0, 2),
        "bias_rows": np.stack([np.asarray(L0_tok_proj_b), np.asarray(L0_attn_bv), np.asarray(L0_attn_bo)]),
        "consts": consts, "rope": rope, "pick": pick, "edge": edge,
    }
    arrays = {n: np.ascontiguousarray(a) for n, a in arrays.items()}
    nc = bacc.Bacc("TRN2", target_bir_lowering=False, num_devices=1)
    args = [nc.dram_tensor(n, a.shape, mybir.dt.from_np(a.dtype), kind="ExternalInput").ap() for n, a in arrays.items()]
    args.append(nc.dram_tensor("out", (T, S, D), F32, kind="ExternalOutput").ap())
    lm_layer(nc, *args)
    return run_bass_kernel_spmd(nc, [arrays], core_ids=[0]).results[0]["out"]
```

```python
from contextlib import ExitStack

import concourse.bass as bass
from concourse import mybir

F32 = mybir.dt.float32
BF16 = mybir.dt.bfloat16
F16 = mybir.dt.float16
I32 = mybir.dt.int32
U32 = mybir.dt.uint32
ALU = mybir.AluOpType
ACT = mybir.ActivationFunctionType
AX = mybir.AxisListType

P = 128
T, S, D = 16, 128, 128
H = 8
HD = D // H
NG = 3
VOCAB = 25000
E = 8
CAP = S // E
SUPER = 4
TPS = 4
SPT = P // T
SPS = SPT * TPS
SINKHORN_ITERS = 8
LN_EPS = 1e-5
GATE_EPS = 1e-6
ROUND = float(3 * 2 ** 22)
NO_ROW = float(2 ** 20)
UP = 64.0
WINDOW = 4

W_PROJ = 0
W_V = W_PROJ + NG * D
W_O = W_V + D
W_Q = W_O + D
W_K = W_Q + D
W_GATE = W_K + D
W_BIAS = W_GATE + E
W_ALL = W_BIAS + 4

C_IDENT = 0
C_GROUP = C_IDENT + P
C_COS = C_GROUP + 8
C_SIN = C_COS + T
C_ALL_OF_ROW = C_SIN + T
C_ROW_OF = C_ALL_OF_ROW + P
C_LATER = C_ROW_OF + T
C_SLOT = C_LATER + P
C_ALL = C_SLOT + CAP


class Chain:

    def __init__(self, eng, sem, per=0):
        self.eng, self.sem, self.per, self.n = eng, sem, per, 0

    def begin(self):
        self.n = 0

    def step(self, ins, k=0):
        self.n += 1
        ins.then_inc(self.sem, 1)
        self.eng.wait_ge(self.sem, k * self.per + self.n)


def wait_freed(eng, sem, count):
    if not (isinstance(count, int) and count == 0):
        eng.wait_ge(sem, count)


def lm_layer(nc, x_win, emb_2, emb_3, emb_4, weights, experts, bias_rows, consts, rope, pick, edge, out):
    with ExitStack() as ctx:
        def sb(name, shape, dt=F32):
            return ctx.enter_context(nc.sbuf_tensor(name, shape, dt))

        def sem(name):
            return ctx.enter_context(nc.semaphore(name))

        def halves(name, shape):
            return [sb(name + "_hi", shape, F16), sb(name + "_lo", shape, F16)]

        w_sb = sb("w_sb", [P, W_ALL])
        c_sb = sb("c_sb", [P, C_ALL])
        rope_h = sb("rope_h", [P, 2, T, 32], F16)
        pick_sb = sb("pick_sb", [P, 2, T * SPS], F16)
        edge_sb = sb("edge_sb", [P, NG, T])
        mean_of = sb("mean_of", [P, P], F16)
        later_bf = sb("later_bf", [P, P], BF16)
        ident_h = sb("ident_h", [P, P], F16)
        exp_sb = sb("exp_sb", [P, E, D])
        exp_h = halves("exp", [P, E, D])
        brow = sb("brow", [P, 3, D])
        brow_h = halves("brow2", [P, 3, D])
        w_h = halves("w", [P, W_BIAS])
        xi = sb("xi", [P, WINDOW, T], I32)
        xf = sb("xf", [P, WINDOW, T])
        gram = sb("gram", [P, NG, T])
        quot = sb("quot", [P, T])
        idx_all = sb("idx_all", [P, T, NG], U32)
        emb = sb("emb", [P, TPS, NG, D])
        embT = halves("embT", [P, TPS, NG * D])
        h = sb("h", [P, TPS, D])
        hb = sb("hb", [P, T, D])
        xn = sb("xn", [P, TPS, D])
        xnT = halves("xnT", [P, SPS, T])
        wq_rot = halves("wq_rot", [P, T, D])
        wk_rot = halves("wk_rot", [P, T, D])
        b_rot = sb("b_rot", [P, 2, T])
        b_rotT = halves("b_rotT", [P, D])
        QT = sb("QT", [P, 2, SPS, T], F16)
        KT = halves("KT", [P, SPS, T])
        V1 = halves("V1", [P, TPS, H, HD + 1])
        Qx = sb("Qx", [P, 2, SPS, H, T], F16)
        smax = sb("smax", [P, SPS])
        prob = sb("prob", [P, SPS, T])
        PT = sb("PT", [P, 2, TPS * H, T], F16)
        Px = sb("Px", [P, 2, TPS * H, SPT, T], F16)
        rden = sb("rden", [P, 2, 2 * H])
        attn = sb("attn", [P, TPS, D])
        attnT = halves("attnT", [P, TPS, D])
        h2 = sb("h2", [P, TPS, D])
        x2 = sb("x2", [P, TPS, D])
        x2T = halves("x2T", [P, T, S])
        stats = sb("stats", [P, 2 * TPS, 6])
        mean, mdiff, var_eps, log_var, rstd0, nwt, rstd, shift_by = (
            sb(n, [P, 2 * TPS]) for n in ("mean", "mdiff", "var_eps", "log_var", "rstd0", "nwt", "rstd", "shift_by"))
        x2s = sb("x2s", [P, T, D])
        x2s_h = halves("x2s2", [P, T, D])
        h2s = sb("h2s", [P, T, D])
        KA = sb("KA", [P, P])
        KAT = sb("KAT", [P, P])
        R = sb("R", [P, T])
        Cj = sb("Cj", [P, T])
        cinv16 = sb("cinv16", [P, T])
        csum = sb("csum", [P, 1])
        cinv = sb("cinv", [P, 1])
        scaled = sb("scaled", [P, P])
        rinv = sb("rinv", [P, P])
        G = sb("G", [P, P])
        G1 = sb("G1", [P, P])
        G2 = sb("G2", [P, P])
        top = sb("top", [P, 2, 8])
        M_bf = sb("M_bf", [P, P], BF16)
        win = sb("win", [P, P])
        pos = sb("pos", [P, P])
        slot = sb("slot", [P, P])
        wgate = sb("wgate", [P, P])
        slotT = sb("slotT", [P, P], F16)
        slot_no = sb("slot_no", [P, CAP], F16)
        gate_tok = sb("gate_tok", [P, T])
        onehot = sb("onehot", [P, T, E, CAP], F16)
        onehotT = sb("onehotT", [P, T, S], F16)
        xg = [sb(f"xg{n}", [P, 2, E, 4, CAP], F16) for n in range(2)]
        yT = sb("yT", [P, 2, 4, E, CAP])
        y = [sb(f"y{n}", [P, 2, 4, D], F16) for n in range(2)]
        res = sb("res", [P, T, D])

        bank = [ctx.enter_context(nc.psum_tensor(f"bank{n}", [P, 512], F32)) for n in range(8)]
        PV, HX, QB, KB, VB, SB, PB = (0, 1), 2, 3, 4, 5, 6, 7
        EMBT = (*PV, QB, KB)

        h2_dram = nc.dram_tensor("h2_scratch", (S * T, D), F32, kind="Internal").ap()
        x2_dram = nc.dram_tensor("x2_scratch", (S * T, D), F32, kind="Internal").ap()

        ident = c_sb[:, C_IDENT:C_IDENT + P]
        group = c_sb[:, C_GROUP:C_GROUP + 8]
        row_of = c_sb[:, C_ROW_OF:C_ROW_OF + T]
        all_of_row = c_sb[:, C_ALL_OF_ROW:C_ALL_OF_ROW + P]

        x_in, c_in, w_in, rope_in, exp_in, brow_in, pick_in = (
            sem(n) for n in ("x_in", "c_in", "w_in", "rope_in", "exp_in", "brow_in", "pick_in"))
        ids_step, idx_ready = sem("ids_step"), sem("idx_ready")
        emb_cleared, pick_cleared = sem("emb_cleared"), sem("pick_cleared")
        gathered = [sem(f"gathered{n}") for n in range(TPS)]
        w_hi, w_lo = sem("w_hi"), sem("w_lo")
        rope_mm, rope_hi, rope_lo, setup_step, setup_done, brotT_done, brotT_hi, brotT_lo = (
            sem(n) for n in ("rope_mm", "rope_hi", "rope_lo", "setup_step", "setup_done", "brotT_done", "brotT_hi",
                             "brotT_lo"))
        embT_done, embT_hi, embT_lo, proj_done = (sem(n) for n in ("embT_done", "embT_hi", "embT_lo", "proj_done"))
        ln_step, var_ready, ln_log, rstd0_ready, shift_ready = (
            sem(n) for n in ("ln_step", "var_ready", "ln_log", "rstd0_ready", "shift_ready"))
        max_done, rden_done = sem("max_done"), sem("rden_done")
        h_ready, hb_done = sem("h_ready"), sem("hb_done")
        xn_ready, xn_ready_a, xnT_done, xnT_hi, xnT_lo = (
            sem(n) for n in ("xn_ready", "xn_ready_a", "xnT_done", "xnT_hi", "xnT_lo"))
        q_done, k_done, v_done = sem("q_done"), sem("k_done"), sem("v_done")
        q_hi, k_hi, v_hi, q_lo, k_lo, v_lo = (sem(n) for n in ("q_hi", "k_hi", "v_hi", "q_lo", "k_lo", "v_lo"))
        qx_v, qx_a = sem("qx_v"), sem("qx_a")
        scores_done, shifted, probs_ready = sem("scores_done"), sem("shifted"), sem("probs_ready")
        PT_done, PT_hi, PT_lo, px_v, px_a = (sem(n) for n in ("PT_done", "PT_hi", "PT_lo", "px_v", "px_a"))
        pv_done, attn_ready, attnT_done, attnT_hi, attnT_lo = (
            sem(n) for n in ("pv_done", "attn_ready", "attnT_done", "attnT_hi", "attnT_lo"))
        wo_done, h2_ready, x2_ready, x2_ready_a, x2T_done, x2T_hi, x2T_lo = (
            sem(n) for n in ("wo_done", "h2_ready", "x2_ready", "x2_ready_a", "x2T_done", "x2T_hi", "x2T_lo"))
        h2_stored, x2_stored, h2s_in, x2s_in = (sem(n) for n in ("h2_stored", "x2_stored", "h2s_in", "x2s_in"))
        x2s_hi, x2s_lo, exp_scaled, exp_hi, exp_lo = (
            sem(n) for n in ("x2s_hi", "x2s_lo", "exp_scaled", "exp_hi", "exp_lo"))
        logits_done, ka_ready, kaT_done, kaT_copied = (
            sem(n) for n in ("logits_done", "ka_ready", "kaT_done", "kaT_copied"))
        r_ready, colsum_done, c_ready, rowsum_done, sink_step = (
            sem(n) for n in ("r_ready", "colsum_done", "c_ready", "rowsum_done", "sink_step"))
        scaled_ready, rowsumB_done, top_step, m_ready, later_done = (
            sem(n) for n in ("scaled_ready", "rowsumB_done", "top_step", "m_ready", "later_done"))
        slot_ready, wg_ready, slotT_done, onehot_ready = (
            sem(n) for n in ("slot_ready", "wg_ready", "slotT_done", "onehot_ready"))
        xg_done, xg_hi, xg_lo, ohT_done, ohT_copied = (
            sem(n) for n in ("xg_done", "xg_hi", "xg_lo", "ohT_done", "ohT_copied"))
        yT_done, yT_copied, y_done, y_hi, y_lo, scat_done, gated = (
            sem(n) for n in ("yT_done", "yT_copied", "y_done", "y_hi", "y_lo", "scat_done", "gated"))
        res_ready = [sem(f"res{c}_ready") for c in range(T // 4)]
        gate_ready, split_done, out_stored = sem("gate_ready"), sem("split_done"), sem("out_stored")

        MASKS_V = 6
        MASKS_QV = 6
        LN_TILES_V = 3
        LN_H, LN_H2, LN_BOTH = slice(0, TPS), slice(TPS, 2 * TPS), slice(0, 2 * TPS)
        CHUNK = 4
        NCH = T // CHUNK
        Y_BANK = (4, 2)
        SCAT_BANK = (5, 0, 1, 5)
        ON_ACT = 1

        class Part:

            def __init__(self, k, n, tiles=(0, TPS), scores_bank=SB, probs_bank=PB):
                self.k, self.n, self.tiles = k, n, range(*tiles)
                self.last = isinstance(k, int) and k >= SUPER - 2 and tiles[1] == TPS
                self.scores_bank, self.probs_bank = bank[scores_bank], bank[probs_bank]
                self.at = slice(tiles[0] * SPT, tiles[1] * SPT)
                self.cols = slice(tiles[0] * P, tiles[1] * P)

        HALVES = [Part(SUPER - 1, SUPER - 1, (0, 2)), Part(SUPER - 1, SUPER, (2, 4), HX, QB)]

        def parts(k):
            return HALVES if isinstance(k, int) and k == SUPER - 1 else [Part(k, k)]

        def x2T_bank(k):
            return bank[PB if not isinstance(k, int) or k < SUPER - 2 else (VB, KB)[k - SUPER + 2]]

        block = ctx.enter_context(nc.Block())

        @block.sync
        def _(sp):
            sp.dma_start(xi[:, :, :], x_win).then_inc(x_in, 16)
            sp.dma_start(edge_sb[:, :, :], edge).then_inc(x_in, 16)
            sp.dma_start(w_sb[:, :], weights).then_inc(w_in, 16)
            sp.dma_start(rope_h[:, :, :, :], rope).then_inc(rope_in, 16)
            sp.dma_start(c_sb[:, :], consts).then_inc(c_in, 16)
            sp.dma_start(brow[:, :, :], bias_rows.partition_broadcast(P)).then_inc(brow_in, 16)
            sp.wait_ge(pick_cleared, 1)
            sp.dma_start(pick_sb[0:2 * T, :, :], pick.rearrange("p n t s -> p n (t s)")).then_inc(pick_in, 16)
            sp.dma_start(exp_sb[:, :, :], experts).then_inc(exp_in, 16)

            def store(k, h2_count):
                rows = slice(k * TPS * P, (k + 1) * TPS * P) if isinstance(k, int) else bass.ds(k * (TPS * P), TPS * P)
                sp.wait_ge(h2_ready, h2_count)
                sp.dma_start(h2_dram[rows, :].rearrange("(i p) d -> p i d", p=P), h2[:, :, :]).then_inc(h2_stored, 16)
                sp.wait_ge(x2_ready, k + 1)
                sp.wait_ge(x2_ready_a, k + 1)
                sp.dma_start(x2_dram[rows, :].rearrange("(i p) d -> p i d", p=P), x2[:, :, :]).then_inc(x2_stored, 16)

            with sp.Fori(0, SUPER - 1) as k:
                store(k, k + 1)
            store(SUPER - 1, HALVES[-1].n + 1)
            sp.wait_ge(x2_stored, 16 * SUPER)
            sp.dma_start(x2s[:, :, :], x2_dram.rearrange("(s t) d -> s t d", t=T)).then_inc(x2s_in, 16)
            sp.wait_ge(h2_stored, 16 * SUPER)
            sp.dma_start(h2s[:, :, :], h2_dram.rearrange("(s t) d -> s t d", t=T)).then_inc(h2s_in, 16)
            for c in range(NCH):
                sp.wait_ge(res_ready[c], 1)
                sp.dma_start(out[c * CHUNK:(c + 1) * CHUNK, :, :].rearrange("b s d -> s b d"),
                             res[:, c * CHUNK:(c + 1) * CHUNK, :]).then_inc(out_stored, 16)
            sp.wait_ge(out_stored, 16 * NCH)

        @block.gpsimd
        def _(pool):
            tables = (emb_2, emb_3, emb_4)

            def gather(k):
                order = [(i, n) for i in range(TPS) for n in range(NG)]
                if k == 0:
                    order[2], order[3] = order[3], order[2]
                for i, n in order:
                    tile = k * TPS + i
                    if k > 0 and n == 0:
                        pool.wait_ge(embT_done, TPS * (k - 1) + i + 1)
                    if tile == T - 1 and n == 0:
                        pool.memset(emb[:, i, :, :], 0.0).then_inc(emb_cleared, 1)
                        pool.wait_ge(emb_cleared, 2)
                    if k == 0 and i == 0:
                        pool.wait_ge(idx_ready, n + 1)
                    pool.indirect_dma_start(
                        emb[:, i, n, :], None, tables[n],
                        bass.IndirectOffsetOnAxis(ap=idx_all[:, tile, n:n + 1], axis=0),
                        bounds_check=VOCAB - 1, oob_is_err=False).then_inc(gathered[i], 16)

            def add_bo(k):
                pool.wait_ge(h_ready, k + 1)
                pool.tensor_tensor(hb[:, k * TPS:(k + 1) * TPS, :], h[:, :, :],
                                   brow[:, 2:3, :].to_broadcast([P, TPS, D]), ALU.add).then_inc(hb_done, 1)

            pool.memset(emb[:, 0, :, :], 0.0).then_inc(emb_cleared, 1)
            pool.wait_ge(emb_cleared, 1)
            pool.memset(pick_sb[:, :, :], 0.0).then_inc(pick_cleared, 1)
            gather(0)
            pool.wait_ge(brow_in, 16)
            gather(1)
            add_bo(0)
            for k in range(2, SUPER):
                gather(k)
                add_bo(k - 1)
            pool.wait_ge(exp_in, 16)
            pool.tensor_scalar(exp_sb[:, :, :], exp_sb[:, :, :], UP, None, ALU.mult).then_inc(exp_scaled, 1)
            add_bo(SUPER - 1)
            pool.wait_ge(exp_hi, 1)
            pool.tensor_tensor(exp_h[1][:, :, :], exp_sb[:, :, :], exp_h[0][:, :, :], ALU.subtract).then_inc(exp_lo, 1)
            pool.wait_ge(c_in, 16)
            pool.tensor_copy(later_bf[:, :], c_sb[:, C_LATER:C_LATER + P])
            pool.tensor_copy(ident_h[:, :], ident).then_inc(split_done, 1)
            pool.wait_ge(x2s_hi, 1)
            pool.tensor_tensor(x2s_h[1][:, :, :], x2s[:, :, :], x2s_h[0][:, :, :], ALU.subtract).then_inc(x2s_lo, 1)
            pool.wait_ge(h2s_in, 16)
            pool.wait_ge(gated, 1)
            rows = slice(ON_ACT * CHUNK, (ON_ACT + 1) * CHUNK)
            pool.tensor_tensor(res[:, rows, :], res[:, rows, :], h2s[:, rows, :], ALU.add).then_inc(res_ready[ON_ACT], 1)

        @block.scalar
        def _(act):
            def guess_rstd(n, cols):
                act.wait_ge(var_ready, n + 1)
                act.activation(log_var[:, cols], var_eps[:, cols], ACT.Ln).then_inc(ln_log, 1)
                act.wait_ge(ln_log, n + 1)
                act.activation(rstd0[:, cols], log_var[:, cols], ACT.Exp, scale=-0.5).then_inc(rstd0_ready, 1)

            def apply(n, cols, src, dst, ready):
                act.wait_ge(shift_ready, n + 1)
                for i in range(LN_TILES_V, TPS):
                    at = cols.start + i
                    ins = act.activation(dst[:, i, :], src[:, i, :], ACT.Identity, bias=shift_by[:, at:at + 1],
                                         scale=rstd[:, at:at + 1])
                ins.then_inc(ready, 1)

            def apply_h2(n, k):
                wait_freed(act, x2_stored, k * 16)
                apply(n, LN_H2, h2, x2, x2_ready_a)

            def embed(k, i):
                act.wait_ge(embT_done, k * TPS + i + 1)
                if not (isinstance(k, int) and k == 0):
                    act.wait_ge(proj_done, (k - 1) * TPS + i + 1)
                act.activation(embT[0][:, i, :], bank[EMBT[i]][:, 0:NG * D], ACT.Copy).then_inc(embT_hi, 1)

            def copy_h(k):
                act.wait_ge(proj_done, TPS * (k + 1))
                wait_freed(act, hb_done, k)
                act.activation(h[:, :, :], bank[HX][:, :].rearrange("p (i d) -> p i d", d=D), ACT.Copy,
                               scale=1 / UP).then_inc(h_ready, 1)

            def copy_xnT(k):
                act.wait_ge(xnT_done, k + 1)
                wait_freed(act, v_done, k)
                act.activation(xnT[0][:, :, :], bank[HX][:, :].rearrange("p (s t) -> p s t", t=T),
                               ACT.Copy).then_inc(xnT_hi, 1)

            def take_q(k):
                act.wait_ge(q_done, k + 1)
                wait_freed(act, qx_v, k)
                act.activation(QT[:, 0, :, :].rearrange("p s t -> p t s"), bank[QB][:, :].rearrange("p (t s) -> p t s", t=T),
                               ACT.Copy).then_inc(q_hi, 1)

            def take_k(k):
                act.wait_ge(k_done, k + 1)
                wait_freed(act, scores_done, k)
                act.activation(KT[0][:, :, :].rearrange("p s t -> p t s"), bank[KB][:, :].rearrange("p (t s) -> p t s", t=T),
                               ACT.Copy).then_inc(k_hi, 1)

            def mask_q(k, g):
                act.wait_ge(q_lo, k + 1)
                act.activation(Qx[:, :, :, g, :], QT[:, :, :, :], ACT.Copy, scale=group[:, g:g + 1]).then_inc(qx_a, 1)

            def take_v(k):
                act.wait_ge(v_done, k + 1)
                wait_freed(act, pv_done, k)
                act.activation(V1[0][:, :, :, 0:HD], bank[VB][:, :].rearrange("p (i g d) -> p i g d", i=TPS, d=HD),
                               ACT.Copy).then_inc(v_hi, 1)

            def exps(k):
                for p in parts(k):
                    act.wait_ge(shifted, p.n + 1)
                    act.activation(prob[:, p.at, :], prob[:, p.at, :], ACT.Exp, scale=1 / UP ** 2).then_inc(probs_ready, 1)

            def take_p(p):
                act.wait_ge(PT_done, p.n + 1)
                wait_freed(act, px_v, p.k)
                act.activation(PT[:, 0, p.at, :], p.probs_bank[:, p.cols].rearrange("p (a t) -> p a t", t=T),
                               ACT.Copy).then_inc(PT_hi, 1)

            def mask_p(p, g):
                act.wait_ge(PT_lo, p.n + 1)
                act.activation(Px[:, :, p.at, g, :], PT[:, :, p.at, :], ACT.Copy, scale=group[:, g:g + 1]).then_inc(px_a, 1)

            def copy_attnT(p):
                act.wait_ge(attnT_done, p.n + 1)
                act.activation(attnT[0][:, p.tiles[0]:p.tiles[-1] + 1, :],
                               p.scores_bank[:, p.cols].rearrange("p (i d) -> p i d", d=D), ACT.Copy).then_inc(attnT_hi, 1)

            def copy_x2T(k):
                act.wait_ge(x2T_done, k + 1)
                dst = x2T[0][:, :, k * SPS:(k + 1) * SPS] if isinstance(k, int) else x2T[0][:, :, bass.ds(k * SPS, SPS)]
                act.activation(dst.rearrange("p t s -> p s t"), x2T_bank(k)[:, :].rearrange("p (s t) -> p s t", t=T),
                               ACT.Copy).then_inc(x2T_hi, 1)

            act.preload_act_table_set("natural_log_exp_and_others")
            act.wait_ge(w_in, 16)
            act.activation(w_h[0][:, :], w_sb[:, 0:W_BIAS], ACT.Copy, scale=UP).then_inc(w_hi, 1)
            act.wait_ge(brow_in, 16)
            act.activation(brow_h[0][:, :, :], brow[:, :, :], ACT.Copy, scale=UP).then_inc(w_hi, 1)

            def take_rope(n, j):
                act.wait_ge(rope_mm, 4 * n + j + 1)
                act.activation((wq_rot, wk_rot)[n][0][:, :, 32 * j:32 * j + 32],
                               bank[4 + j][:, :].rearrange("p (t c) -> p t c", c=32), ACT.Copy,
                               scale=HD ** -0.5 if n == 0 else 1.0).then_inc(rope_hi, 1)

            for j in range(4):
                take_rope(0, j)
            act.wait_ge(brotT_done, 1)
            act.activation(b_rotT[0][0:2 * T, :], bank[VB][0:2 * T, 0:D], ACT.Copy).then_inc(brotT_hi, 1)
            for i in range(TPS):
                embed(0, i)
            copy_h(0)
            take_rope(1, 0)
            guess_rstd(0, LN_H)
            take_rope(1, 1)
            apply(0, LN_H, h, xn, xn_ready_a)
            take_rope(1, 2)
            take_rope(1, 3)
            copy_xnT(0)

            take_q(0)
            take_k(0)
            mask_q(0, 6)
            mask_q(0, 7)
            take_v(0)
            embed(1, 0)
            embed(1, 1)
            embed(1, 2)
            embed(1, 3)
            exps(0)
            take_p(Part(0, 0))
            copy_h(1)
            guess_rstd(1, LN_H)
            mask_p(Part(0, 0), 6)
            apply(1, LN_H, h, xn, xn_ready_a)
            mask_p(Part(0, 0), 7)
            copy_xnT(1)
            take_q(1)
            take_k(1)
            mask_q(1, 6)
            mask_q(1, 7)
            take_v(1)
            copy_attnT(Part(0, 0))
            embed(2, 0)
            embed(2, 1)
            embed(2, 2)
            embed(2, 3)
            copy_h(2)
            guess_rstd(2, LN_BOTH)
            apply(2, LN_H, h, xn, xn_ready_a)
            exps(1)
            copy_xnT(2)

            def supertile(k, emb_next):
                p = Part(k, k)
                take_p(p)
                apply_h2(k + 1, k - 1)
                mask_p(p, 6)
                take_q(k + 1)
                mask_p(p, 7)
                take_k(k + 1)
                mask_q(k + 1, 6)
                mask_q(k + 1, 7)
                copy_x2T(k - 1)
                copy_attnT(p)
                take_v(k + 1)
                if emb_next:
                    embed(k + 2, 0)
                    embed(k + 2, 1)
                    embed(k + 2, 2)
                    embed(k + 2, 3)
                    copy_h(k + 2)
                guess_rstd(k + 2, LN_BOTH if emb_next else LN_H2)
                if emb_next:
                    apply(k + 2, LN_H, h, xn, xn_ready_a)
                exps(k + 1)
                if emb_next:
                    copy_xnT(k + 2)

            with act.Fori(1, SUPER - 2) as k:
                supertile(k, True)
            supertile(SUPER - 2, False)

            first, second = HALVES
            take_p(first)
            take_p(second)
            mask_p(first, 6)
            mask_p(first, 7)
            mask_p(second, 6)
            mask_p(second, 7)
            apply_h2(SUPER, SUPER - 2)
            copy_attnT(first)
            copy_attnT(second)
            act.wait_ge(exp_scaled, 1)
            act.activation(exp_h[0][:, :, :], exp_sb[:, :, :], ACT.Copy).then_inc(exp_hi, 1)
            copy_x2T(SUPER - 2)
            guess_rstd(SUPER + 1, LN_H2)
            apply_h2(SUPER + 1, SUPER - 1)
            copy_x2T(SUPER - 1)

            act.wait_ge(kaT_done, 1)
            act.activation(KAT[:, :], bank[1][:, 0:P], ACT.Copy).then_inc(kaT_copied, 1)
            act.wait_ge(x2s_in, 16)
            act.activation(x2s_h[0][:, :, :], x2s[:, :, :], ACT.Copy).then_inc(x2s_hi, 1)
            for step in range(NCH + 2):
                if step < NCH:
                    c = step
                    act.wait_ge(xg_done, c + 1)
                    if c >= 2:
                        act.wait_ge(yT_done, c - 1)
                    act.activation(xg[0][:, c % 2, :, :, :].rearrange("p e b j -> p b e j"),
                                   bank[0][:, :].rearrange("p (b e j) -> p b e j", b=CHUNK, e=E),
                                   ACT.Copy).then_inc(xg_hi, 1)
                    act.wait_ge(ohT_done, c + 1)
                    act.activation(onehotT[:, c * CHUNK:(c + 1) * CHUNK, :],
                                   bank[6 + c % 2][:, 0:256].bitcast(F16).rearrange("p (b s) -> p b s", b=CHUNK),
                                   ACT.Copy).then_inc(ohT_copied, 1)
                if 1 <= step <= NCH:
                    c = step - 1
                    act.wait_ge(yT_done, c + 1)
                    act.activation(yT[:, c % 2, :, :, :].rearrange("p b e j -> p e b j"),
                                   bank[3][:, :].rearrange("p (e b j) -> p e b j", b=CHUNK, e=E),
                                   ACT.Copy).then_inc(yT_copied, 1)
                if 2 <= step:
                    c = step - 2
                    act.wait_ge(y_done, c + 1)
                    if c >= 2:
                        act.wait_ge(scat_done, c - 1)
                    act.activation(y[0][:, c % 2, :, :], bank[Y_BANK[c % 2]][:, :].rearrange("p (b d) -> p b d", b=CHUNK),
                                   ACT.Copy).then_inc(y_hi, 1)
            act.wait_ge(scat_done, ON_ACT + 1)
            act.wait_ge(gate_ready, 1)
            for b in range(CHUNK):
                row = ON_ACT * CHUNK + b
                ins = act.activation(res[:, row, :], bank[SCAT_BANK[ON_ACT]][:, b * D:(b + 1) * D], ACT.Copy,
                                     scale=gate_tok[:, row:row + 1])
            ins.then_inc(gated, 1)

        @block.tensor
        def _(pe):
            def product(dst, w, x, start=True, stop=True):
                pe.matmul(dst, w[0], x[0], start=start, stop=False)
                pe.matmul(dst, w[0], x[1], start=False, stop=False)
                return pe.matmul(dst, w[1], x[0], start=False, stop=stop)

            def bias(dst, n):
                for part in range(2):
                    pe.matmul(dst, mean_of[:, :], brow_h[part][:, n:n + 1, :].to_broadcast([P, TPS, D]),
                              start=(part == 0), stop=False)

            def rope(n, j):
                if n == 1:
                    pe.wait_ge(rope_lo, j + 1)
                rows, w0 = slice(32 * j, 32 * j + 32), (W_Q, W_K)[n]
                product(bank[4 + j][:, :], [w_h[part][rows, w0:w0 + D] for part in range(2)],
                        [rope_h[rows, part, :, :] for part in range(2)]).then_inc(rope_mm, 1)

            def turn(k, i):
                pe.wait_ge(gathered[i], (k + 1) * (16 * NG))
                if i < 2:
                    if not isinstance(k, int) or k > 1:
                        pe.wait_ge(attn_ready, k - 1)
                else:
                    wait_freed(pe, (q_lo, k_lo)[i - 2], k)
                for n in range(NG):
                    ins = pe.transpose(bank[EMBT[i]][:, n * D:(n + 1) * D], emb[:, i, n, :], ident)
                ins.then_inc(embT_done, 1)

            def project(k, i):
                if i == 0:
                    wait_freed(pe, xnT_lo, k)
                    bias(bank[HX][:, :], 0)
                pe.wait_ge(embT_hi, k * TPS + i + 1)
                pe.wait_ge(embT_lo, k * TPS + i + 1)
                for n in range(NG):
                    ins = product(bank[HX][:, i * D:(i + 1) * D],
                                  [embT[part][:, i, n * D:(n + 1) * D] for part in range(2)],
                                  [w_h[part][:, W_PROJ + n * D:W_PROJ + (n + 1) * D] for part in range(2)],
                                  start=False, stop=(i == TPS - 1 and n == NG - 1))
                ins.then_inc(proj_done, 1)

            def transpose_xn(k):
                pe.wait_ge(xn_ready, k + 1)
                for i in range(TPS):
                    if i == LN_TILES_V:
                        pe.wait_ge(xn_ready_a, k + 1)
                    ins = pe.transpose(bank[HX][:, i * D:(i + 1) * D], xn[:, i, :], ident)
                ins.then_inc(xnT_done, 1)

            def rotated(k, n, b, w, done):
                for part in range(2):
                    pe.matmul(bank[b][:, :], b_rotT[part][:, :], pick_sb[:, n, :], start=(part == 0), stop=False)
                for t in range(T):
                    for part in range(2):
                        pe.matmul(bank[b][:, t * SPS:(t + 1) * SPS], w[part][:, t, :], xnT[0][:, :, t],
                                  start=False, stop=False)
                pe.wait_ge(xnT_lo, k + 1)
                for t in range(T):
                    ins = pe.matmul(bank[b][:, t * SPS:(t + 1) * SPS], w[0][:, t, :], xnT[1][:, :, t],
                                    start=False, stop=(t == T - 1))
                ins.then_inc(done, 1)

            def query(k):
                pe.wait_ge(xnT_hi, k + 1)
                rotated(k, 0, QB, wq_rot, q_done)

            def key(k):
                rotated(k, 1, KB, wk_rot, k_done)

            def value(k):
                wait_freed(pe, v_lo, k)
                bias(bank[VB][:, :], 1)
                for i in range(TPS):
                    ins = product(bank[VB][:, i * D:(i + 1) * D],
                                  [xnT[part][:, i * SPT:(i + 1) * SPT, :].rearrange("p s t -> p (s t)") for part in range(2)],
                                  [w_h[part][:, W_V:W_V + D] for part in range(2)], start=False, stop=(i == TPS - 1))
                ins.then_inc(v_done, 1)

            def scores(k):
                for p in parts(k):
                    scores_part(p)

            def scores_part(p):
                k = p.k
                pe.wait_ge(k_lo, k + 1)
                pe.wait_ge(qx_v, k + 1)
                pe.wait_ge(qx_a, (k + 1) * (H - MASKS_QV))
                wait_freed(pe, attnT_lo, k)
                for s in range(p.at.start, p.at.stop):
                    ins = product(p.scores_bank[:, s * T:(s + 1) * T],
                                  [Qx[:, part, s, :, :].rearrange("p g t -> p (g t)") for part in range(2)],
                                  [KT[part][:, s, :] for part in range(2)])
                ins.then_inc(scores_done, 1)

            def transpose_x2(k):
                if isinstance(k, int) and k == SUPER - 1:
                    pe.wait_ge(k_lo, SUPER)
                elif isinstance(k, int) and k == SUPER - 2:
                    pe.wait_ge(v_lo, SUPER)
                else:
                    pe.wait_ge(PT_lo, k + 2)
                pe.wait_ge(x2_ready, k + 1)
                for i in range(TPS):
                    if i == LN_TILES_V:
                        pe.wait_ge(x2_ready_a, k + 1)
                    ins = pe.transpose(x2T_bank(k)[:, i * D:(i + 1) * D], x2[:, i, :], ident)
                ins.then_inc(x2T_done, 1)

            def transpose_prob(p):
                pe.wait_ge(probs_ready, p.n + 1)
                wait_freed(pe, h2_ready, p.k)
                for i in p.tiles:
                    ins = pe.transpose(p.probs_bank[:, i * P:(i + 1) * P],
                                       prob[:, i * SPT:(i + 1) * SPT, :].rearrange("p s t -> p (s t)"), ident)
                ins.then_inc(PT_done, 1)

            def weigh_v(p):
                pe.wait_ge(px_v, p.n + 1)
                pe.wait_ge(px_a, (p.n + 1) * (SPT - MASKS_V))
                pe.wait_ge(v_lo, p.k + 1)
                for i in p.tiles:
                    for g in range(H):
                        at = ((i % 2) * H + g) * (HD + 1)
                        ins = product(bank[PV[i // 2]][:, at:at + HD + 1],
                                      [Px[:, part, i * H + g, :, :].rearrange("p s t -> p (s t)") for part in range(2)],
                                      [V1[part][:, i, g, :] for part in range(2)])
                ins.then_inc(pv_done, 1)

            def transpose_attn(p):
                pe.wait_ge(attn_ready, p.n + 1)
                for i in p.tiles:
                    ins = pe.transpose(p.scores_bank[:, i * D:(i + 1) * D], attn[:, i, :], ident)
                ins.then_inc(attnT_done, 1)

            def project_out(p):
                pe.wait_ge(attnT_hi, p.n + 1)
                wait_freed(pe, x2T_lo, min(p.k, SUPER - 2) if isinstance(p.k, int) else p.k)
                for i in p.tiles:
                    for part in range(2):
                        pe.matmul(p.probs_bank[:, i * D:(i + 1) * D], attnT[0][:, i, :], w_h[part][:, W_O:W_O + D],
                                  start=(part == 0 and i == p.tiles[0]), stop=False)
                pe.wait_ge(attnT_lo, p.n + 1)
                for i in p.tiles:
                    ins = pe.matmul(p.probs_bank[:, i * D:(i + 1) * D], attnT[1][:, i, :], w_h[0][:, W_O:W_O + D],
                                    start=False, stop=(i == p.tiles[-1]))
                ins.then_inc(wo_done, 1)

            pe.wait_ge(w_lo, 1)
            pe.wait_ge(rope_in, 16)
            for j in range(4):
                rope(0, j)
            pe.wait_ge(c_in, 16)
            pe.wait_ge(setup_done, 1)
            pe.wait_ge(rope_lo, 2)
            pe.transpose(bank[VB][0:2 * T, 0:D], b_rot[:, :, :].rearrange("p n t -> p (n t)"), ident).then_inc(brotT_done, 1)
            pe.wait_ge(w_lo, 2)
            for i in range(TPS):
                turn(0, i)
                if i > 0:
                    project(0, i - 1)
            project(0, TPS - 1)
            pe.wait_ge(brotT_lo, 1)
            for j in range(4):
                rope(1, j)
            transpose_xn(0)
            pe.wait_ge(rope_lo, 8)
            pe.wait_ge(pick_in, 16)

            query(0)
            key(0)
            value(0)
            turn(1, 0)
            turn(1, 1)
            turn(1, 2)
            turn(1, 3)
            scores(0)
            project(1, 0)
            project(1, 1)
            transpose_prob(Part(0, 0))
            project(1, 2)
            project(1, 3)
            transpose_xn(1)
            weigh_v(Part(0, 0))
            query(1)
            key(1)
            value(1)
            transpose_attn(Part(0, 0))
            turn(2, 0)
            turn(2, 1)
            turn(2, 2)
            turn(2, 3)
            project_out(Part(0, 0))
            project(2, 0)
            project(2, 1)
            project(2, 2)
            project(2, 3)
            scores(1)
            transpose_xn(2)

            def supertile(k, emb_next):
                p = Part(k, k)
                transpose_prob(p)
                query(k + 1)
                key(k + 1)
                weigh_v(p)
                value(k + 1)
                transpose_x2(k - 1)
                transpose_attn(p)
                if emb_next:
                    turn(k + 2, 0)
                    turn(k + 2, 1)
                    turn(k + 2, 2)
                    turn(k + 2, 3)
                project_out(p)
                if emb_next:
                    project(k + 2, 0)
                    project(k + 2, 1)
                    project(k + 2, 2)
                    project(k + 2, 3)
                scores(k + 1)
                if emb_next:
                    transpose_xn(k + 2)

            with pe.Fori(1, SUPER - 2) as k:
                supertile(k, True)
            supertile(SUPER - 2, False)

            first, second = HALVES
            transpose_prob(first)
            transpose_prob(second)
            weigh_v(first)
            weigh_v(second)
            transpose_attn(first)
            transpose_attn(second)
            project_out(first)
            project_out(second)
            transpose_x2(SUPER - 2)
            transpose_x2(SUPER - 1)

            gate = [w_h[part][:, W_GATE:W_GATE + E] for part in range(2)]
            pe.wait_ge(x2T_hi, SUPER)
            for b in range(T):
                pe.matmul(bank[0][:, b * E:(b + 1) * E], x2T[0][:, b, :], gate[0], start=(b == 0), stop=False)
                pe.matmul(bank[0][:, b * E:(b + 1) * E], x2T[0][:, b, :], gate[1], start=False, stop=False)
            pe.wait_ge(x2T_lo, SUPER)
            for b in range(T):
                ins = pe.matmul(bank[0][:, b * E:(b + 1) * E], x2T[1][:, b, :], gate[0], start=False, stop=(b == T - 1))
            ins.then_inc(logits_done, 1)
            pe.wait_ge(ka_ready, 1)
            pe.wait_ge(r_ready, 1)
            pe.matmul(bank[2][:, 0:T], KA[:, :], R[:, :], start=True, stop=True).then_inc(colsum_done, 1)
            pe.transpose(bank[1][:, 0:P], KA[:, :], ident).then_inc(kaT_done, 1)
            pe.wait_ge(kaT_copied, 1)
            with pe.Fori(0, SINKHORN_ITERS - 1) as n:
                pe.wait_ge(c_ready, n + 1)
                pe.matmul(bank[3][:, 0:T], KAT[:, :], Cj[:, :], start=True, stop=True).then_inc(rowsum_done, 1)
                pe.wait_ge(r_ready, n + 2)
                pe.matmul(bank[2][:, 0:T], KA[:, :], R[:, :], start=True, stop=True).then_inc(colsum_done, 1)
            pe.wait_ge(scaled_ready, 1)
            pe.matmul(bank[3][:, 0:P], scaled[:, :], KAT[:, :], start=True, stop=True).then_inc(rowsumB_done, 1)
            pe.wait_ge(split_done, 1)
            pe.wait_ge(m_ready, 1)
            pe.matmul(bank[4][:, 0:P], later_bf[:, :], M_bf[:, :], start=True, stop=True).then_inc(later_done, 1)
            pe.wait_ge(slot_ready, 1)
            pe.transpose(bank[5][:, 0:P], slot[:, :], ident).then_inc(slotT_done, 1)
            pe.wait_ge(wg_ready, 1)
            pe.transpose(bank[6][:, 0:P], wgate[:, :], ident).then_inc(slotT_done, 1)

            pe.wait_ge(split_done, 1)
            pe.wait_ge(x2s_hi, 1)
            pe.wait_ge(x2s_lo, 1)
            pe.wait_ge(exp_hi, 1)
            pe.wait_ge(exp_lo, 1)
            ohT_bank = [bank[6 + n][:, 0:256].bitcast(F16) for n in range(2)]

            def gather(c):
                pe.wait_ge(onehot_ready, c + 1)
                if c >= 1:
                    pe.wait_ge(xg_hi, c)
                    pe.wait_ge(xg_lo, c)
                for part in range(2):
                    for b in range(CHUNK):
                        ins = pe.matmul(bank[part][:, b * P:(b + 1) * P], x2s_h[part][:, c * CHUNK + b, :],
                                        onehot[:, c * CHUNK + b, :, :], start=True, stop=True)
                ins.then_inc(xg_done, 1)
                if c == 0:
                    pe.wait_ge(gate_ready, 1)
                if c >= 2:
                    pe.wait_ge(ohT_copied, c - 1)
                for b in range(CHUNK):
                    ins = pe.transpose(ohT_bank[c % 2][:, b * P:(b + 1) * P],
                                       onehot[:, c * CHUNK + b, :, :].rearrange("p e j -> p (e j)"), ident_h[:, :])
                ins.then_inc(ohT_done, 1)

            def apply_experts(c):
                pe.wait_ge(xg_hi, c + 1)
                pe.wait_ge(xg_lo, c + 1)
                if c >= 1:
                    pe.wait_ge(yT_copied, c)
                w = CHUNK * CAP
                for e in range(E):
                    ins = product(bank[3][:, e * w:(e + 1) * w], [exp_h[part][:, e, :] for part in range(2)],
                                  [xg[part][:, c % 2, e, :, :] for part in range(2)])
                ins.then_inc(yT_done, 1)

            def turn_y(c):
                pe.wait_ge(yT_copied, c + 1)
                if c >= 2:
                    pe.wait_ge(y_lo, c - 1)
                for b in range(CHUNK):
                    ins = pe.transpose(bank[Y_BANK[c % 2]][:, b * P:(b + 1) * P],
                                       yT[:, c % 2, b, :, :].rearrange("p e j -> p (e j)"), ident)
                ins.then_inc(y_done, 1)

            def scatter(c):
                pe.wait_ge(y_hi, c + 1)
                pe.wait_ge(y_lo, c + 1)
                pe.wait_ge(ohT_copied, c + 1)
                if c == NCH - 1:
                    pe.wait_ge(res_ready[0], 1)
                for b in range(CHUNK):
                    for part in range(2):
                        ins = pe.matmul(bank[SCAT_BANK[c]][:, b * D:(b + 1) * D], onehotT[:, c * CHUNK + b, :],
                                        y[part][:, c % 2, b, :], start=(part == 0), stop=(part == 1))
                ins.then_inc(scat_done, 1)

            for step in range(NCH + 3):
                if step < NCH:
                    gather(step)
                if 1 <= step <= NCH:
                    apply_experts(step - 1)
                if 2 <= step <= NCH + 1:
                    turn_y(step - 2)
                if 3 <= step:
                    scatter(step - 3)

        @block.vector
        def _(dve):
            ids = Chain(dve, ids_step)

            def mod_vocab(v):
                ids.step(dve.tensor_scalar(quot[:, :], v, 1.0 / VOCAB, 0.5 / VOCAB - 0.5, ALU.mult, ALU.add))
                ids.step(dve.tensor_scalar(quot[:, :], quot[:, :], ROUND, -ROUND, ALU.add, ALU.add))
                ids.step(dve.scalar_tensor_tensor(v, quot[:, :], -float(VOCAB), v, ALU.mult, ALU.add))

            def emit(n):
                dve.tensor_tensor(idx_all[:, :, n], gram[:, n, :], edge_sb[:, n, :], ALU.add).then_inc(idx_ready, 1)

            def shift_in(dst, prev, byte):
                ids.step(dve.scalar_tensor_tensor(dst, prev, 64.0, byte, ALU.mult, ALU.add))

            dve.wait_ge(x_in, 32)
            ids.step(dve.tensor_copy(xf[:, :, :], xi[:, :, :]))
            shift_in(gram[:, 0, :], xf[:, 1, :], xf[:, 2, :])
            emit(0)
            shift_in(gram[:, 1, :], gram[:, 0, :], xf[:, 3, :])
            mod_vocab(gram[:, 1, :])
            emit(1)
            shift_in(gram[:, 2, :], xf[:, 0, :], xf[:, 1, :])
            shift_in(gram[:, 2, :], gram[:, 2, :], xf[:, 2, :])
            mod_vocab(gram[:, 2, :])
            shift_in(gram[:, 2, :], gram[:, 2, :], xf[:, 3, :])
            mod_vocab(gram[:, 2, :])
            emit(2)

            setup = Chain(dve, setup_step)
            dve.memset(R[:, :], 1.0).then_inc(r_ready, 1)
            setup.step(dve.memset(mean_of[:, :], 1.0 / P))
            for part, value in ((0, 1.0), (1, 0.0)):
                setup.step(dve.memset(V1[part][:, :, :, HD:HD + 1], value))
                setup.step(dve.memset(b_rotT[part][:, :], 0.0))
            dve.wait_ge(w_in, 16)
            dve.wait_ge(w_hi, 1)
            dve.scalar_tensor_tensor(w_h[1][:, :], w_sb[:, 0:W_BIAS], UP, w_h[0][:, :], ALU.mult,
                                     ALU.subtract).then_inc(w_lo, 1)
            dve.wait_ge(brow_in, 16)
            dve.wait_ge(w_hi, 2)
            dve.scalar_tensor_tensor(brow_h[1][:, :, :], brow[:, :, :], UP, brow_h[0][:, :, :], ALU.mult,
                                     ALU.subtract).then_inc(w_lo, 1)
            dve.wait_ge(c_in, 16)
            dve.tensor_copy(slot_no[:, :], c_sb[:, C_SLOT:C_SLOT + CAP])
            for n, scale in ((0, UP * HD ** -0.5), (1, UP)):
                setup.step(dve.tensor_scalar(b_rot[:, n, :], c_sb[:, C_COS:C_COS + T],
                                             w_sb[:, W_BIAS + n:W_BIAS + n + 1], scale, ALU.mult, ALU.mult))
                setup.step(dve.tensor_scalar(rden[:, n, :], c_sb[:, C_SIN:C_SIN + T],
                                             w_sb[:, W_BIAS + 2 + n:W_BIAS + 3 + n], scale, ALU.mult, ALU.mult))
                ins = dve.tensor_tensor(b_rot[:, n, :], b_rot[:, n, :], rden[:, n, :], ALU.add)
            ins.then_inc(setup_done, 1)

            def ln_stats(src, cols, tiles=range(TPS)):
                for i in tiles:
                    ins = dve.bn_stats(stats[:, cols.start + i, :], src[:, i, :])
                return ins

            def ln_variance(n, cols):
                even, odd = stats[:, cols, 1], stats[:, cols, 4]
                dve.wait_ge(ln_step, n * LN_STEPS + 1)
                dve.tensor_tensor(mean[:, cols], even, odd, ALU.add)
                dve.tensor_tensor(mdiff[:, cols], even, odd, ALU.subtract)
                dve.tensor_tensor(var_eps[:, cols], stats[:, cols, 2], stats[:, cols, 5], ALU.add).then_inc(ln_step, 1)
                dve.wait_ge(ln_step, n * LN_STEPS + 2)
                dve.tensor_scalar(mean[:, cols], mean[:, cols], 0.5, None, ALU.mult)
                dve.tensor_scalar(var_eps[:, cols], var_eps[:, cols], 1.0 / D, LN_EPS, ALU.mult, ALU.add)
                dve.scalar_tensor_tensor(mdiff[:, cols], mdiff[:, cols], 0.25, mdiff[:, cols], ALU.mult, ALU.mult)\
                    .then_inc(ln_step, 1)
                dve.wait_ge(ln_step, n * LN_STEPS + 3)
                dve.tensor_tensor(var_eps[:, cols], var_eps[:, cols], mdiff[:, cols], ALU.add).then_inc(var_ready, 1)

            def ln_refine(n, cols):
                dve.wait_ge(rstd0_ready, n + 1)
                dve.scalar_tensor_tensor(nwt[:, cols], rstd0[:, cols], -0.5, rstd0[:, cols], ALU.mult, ALU.mult)\
                    .then_inc(ln_step, 1)
                dve.wait_ge(ln_step, n * LN_STEPS + 4)
                dve.tensor_tensor(nwt[:, cols], nwt[:, cols], var_eps[:, cols], ALU.mult).then_inc(ln_step, 1)
                dve.wait_ge(ln_step, n * LN_STEPS + 5)
                dve.scalar_tensor_tensor(rstd[:, cols], nwt[:, cols], 1.5, rstd0[:, cols], ALU.add, ALU.mult)\
                    .then_inc(ln_step, 1)
                dve.wait_ge(ln_step, n * LN_STEPS + 6)
                dve.scalar_tensor_tensor(shift_by[:, cols], mean[:, cols], -1.0, rstd[:, cols], ALU.mult, ALU.mult)\
                    .then_inc(shift_ready, 1)

            def ln_apply(cols, src, dst, ready):
                for i in range(LN_TILES_V):
                    at = cols.start + i
                    ins = dve.tensor_scalar(dst[:, i, :], src[:, i, :], mean[:, at:at + 1], rstd[:, at:at + 1],
                                            ALU.subtract, ALU.mult)
                ins.then_inc(ready, 1)

            LN_STEPS = 6

            def apply_h2(k):
                wait_freed(dve, x2_stored, k * 16)
                ln_apply(LN_H2, h2, x2, x2_ready)

            def low(dst, src, hi, hi_ready, count, ready):
                dve.wait_ge(hi_ready, count)
                dve.tensor_tensor(dst, src, hi, ALU.subtract).then_inc(ready, 1)

            def embed(k, i):
                low(embT[1][:, i, :], bank[EMBT[i]][:, 0:NG * D], embT[0][:, i, :], embT_hi, k * TPS + i + 1, embT_lo)

            def stats_h(k):
                dve.wait_ge(h_ready, k + 1)
                ln_stats(h, LN_H).then_inc(ln_step, 1)

            def take_xnT(k):
                low(xnT[1][:, :, :], bank[HX][:, :].rearrange("p (s t) -> p s t", t=T), xnT[0][:, :, :],
                    xnT_hi, k + 1, xnT_lo)

            def take_q(k):
                wait_freed(dve, qx_a, k * (H - MASKS_QV))
                low(QT[:, 1, :, :].rearrange("p s t -> p t s"), bank[QB][:, :].rearrange("p (t s) -> p t s", t=T),
                    QT[:, 0, :, :].rearrange("p s t -> p t s"), q_hi, k + 1, q_lo)

            def mask_q(k, heads):
                dve.wait_ge(q_lo, k + 1)
                wait_freed(dve, scores_done, k)
                for g in heads:
                    ins = dve.tensor_scalar(Qx[:, :, :, g, :], QT[:, :, :, :], group[:, g:g + 1], None, ALU.mult)
                if MASKS_QV - 1 in heads:
                    ins.then_inc(qx_v, 1)

            def take_k(k):
                low(KT[1][:, :, :].rearrange("p s t -> p t s"), bank[KB][:, :].rearrange("p (t s) -> p t s", t=T),
                    KT[0][:, :, :].rearrange("p s t -> p t s"), k_hi, k + 1, k_lo)

            def take_v(k):
                low(V1[1][:, :, :, 0:HD], bank[VB][:, :].rearrange("p (i g d) -> p i g d", i=TPS, d=HD),
                    V1[0][:, :, :, 0:HD], v_hi, k + 1, v_lo)

            def maximum(p):
                dve.wait_ge(scores_done, p.n + 1)
                dve.tensor_reduce(smax[:, p.at], p.scores_bank[:, p.cols].rearrange("p (s t) -> p s t", t=T), AX.X,
                                  ALU.max).then_inc(max_done, 1)

            def subtract_max(p):
                dve.wait_ge(max_done, p.n + 1)
                dve.tensor_tensor(prob[:, p.at, :], p.scores_bank[:, p.cols].rearrange("p (s t) -> p s t", t=T),
                                  smax[:, p.at].unsqueeze(2).to_broadcast([P, p.at.stop - p.at.start, T]),
                                  ALU.subtract).then_inc(shifted, 1)

            def take_p(p):
                wait_freed(dve, px_a, p.k * (SPT - MASKS_V))
                low(PT[:, 1, p.at, :], p.probs_bank[:, p.cols].rearrange("p (a t) -> p a t", t=T), PT[:, 0, p.at, :],
                    PT_hi, p.n + 1, PT_lo)

            def mask_p(p, positions):
                dve.wait_ge(PT_lo, p.n + 1)
                for g in positions:
                    ins = dve.tensor_scalar(Px[:, :, p.at, g, :], PT[:, :, p.at, :], group[:, g:g + 1], None, ALU.mult)
                if MASKS_V - 1 in positions:
                    ins.then_inc(px_v, 1)

            def normalise(p):
                dve.wait_ge(pv_done, p.n + 1)
                pairs = [(n, bank[PV[n]][:, 0:2 * H * (HD + 1)].rearrange("p (a d) -> p a d", d=HD + 1))
                         for n in sorted({i // 2 for i in p.tiles})]
                for n, o in pairs:
                    ins = dve.reciprocal(rden[:, n, :], o[:, :, HD])
                ins.then_inc(rden_done, 1)
                dve.wait_ge(rden_done, p.n + 1)
                for n, o in pairs:
                    ins = dve.tensor_tensor(attn[:, 2 * n:2 * n + 2, :].rearrange("p i (g d) -> p (i g) d", d=HD),
                                            o[:, :, 0:HD], rden[:, n, :].unsqueeze(2).to_broadcast([P, 2 * H, HD]),
                                            ALU.mult)
                ins.then_inc(attn_ready, 1)

            def take_attnT(p):
                tiles = slice(p.tiles[0], p.tiles[-1] + 1)
                low(attnT[1][:, tiles, :], p.scores_bank[:, p.cols].rearrange("p (i d) -> p i d", d=D),
                    attnT[0][:, tiles, :], attnT_hi, p.n + 1, attnT_lo)

            def residual(p):
                k, lo, n = p.k, p.tiles[0], len(p.tiles)
                dve.wait_ge(wo_done, p.n + 1)
                dve.wait_ge(hb_done, k + 1)
                wait_freed(dve, h2_stored, k * 16)
                wait_freed(dve, x2_ready_a, k)
                src = hb[:, k * TPS + lo:k * TPS + lo + n, :] if isinstance(k, int) else hb[:, bass.ds(k * TPS, TPS), :]
                dve.scalar_tensor_tensor(h2[:, lo:lo + n, :], p.probs_bank[:, p.cols].rearrange("p (i d) -> p i d", d=D),
                                         1 / UP ** 2, src, ALU.mult, ALU.add).then_inc(h2_ready, 1)

            def stats_h2(p):
                dve.wait_ge(h2_ready, p.n + 1)
                ins = ln_stats(h2, LN_H2, p.tiles)
                if p.last:
                    ins.then_inc(ln_step, 1)

            def take_rope(n, j):
                dve.wait_ge(rope_hi, 4 * n + j + 1)
                w = (wq_rot, wk_rot)[n]
                dve.scalar_tensor_tensor(w[1][:, :, 32 * j:32 * j + 32],
                                         bank[4 + j][:, :].rearrange("p (t c) -> p t c", c=32),
                                         HD ** -0.5 if n == 0 else 1.0,
                                         w[0][:, :, 32 * j:32 * j + 32], ALU.mult, ALU.subtract).then_inc(rope_lo, 1)

            for j in range(4):
                take_rope(0, j)
            dve.wait_ge(brotT_hi, 1)
            dve.tensor_tensor(b_rotT[1][0:2 * T, :], bank[VB][0:2 * T, 0:D], b_rotT[0][0:2 * T, :],
                              ALU.subtract).then_inc(brotT_lo, 1)
            for i in range(TPS):
                embed(0, i)
            stats_h(0)
            ln_variance(0, LN_H)
            take_rope(1, 0)
            ln_refine(0, LN_H)
            ln_apply(LN_H, h, xn, xn_ready)
            for j in range(1, 4):
                take_rope(1, j)

            def take_x2T(k):
                cols = slice(k * SPS, (k + 1) * SPS) if isinstance(k, int) else bass.ds(k * SPS, SPS)
                low(x2T[1][:, :, cols].rearrange("p t s -> p s t"), x2T_bank(k)[:, :].rearrange("p (s t) -> p s t", t=T),
                    x2T[0][:, :, cols].rearrange("p t s -> p s t"), x2T_hi, k + 1, x2T_lo)

            take_xnT(0)
            take_q(0)
            mask_q(0, (0, 1))
            mask_q(0, (2, 3))
            mask_q(0, (4, 5))
            take_k(0)
            take_v(0)
            embed(1, 0)
            embed(1, 1)
            embed(1, 2)
            embed(1, 3)
            maximum(Part(0, 0))
            subtract_max(Part(0, 0))
            take_p(Part(0, 0))
            stats_h(1)
            ln_variance(1, LN_H)
            mask_p(Part(0, 0), (0, 1))
            ln_refine(1, LN_H)
            ln_apply(LN_H, h, xn, xn_ready)
            mask_p(Part(0, 0), (2, 3))
            mask_p(Part(0, 0), (4, 5))
            take_xnT(1)
            take_q(1)
            mask_q(1, (0, 1))
            mask_q(1, (2, 3))
            mask_q(1, (4, 5))
            normalise(Part(0, 0))
            take_k(1)
            take_attnT(Part(0, 0))
            embed(2, 0)
            embed(2, 1)
            embed(2, 2)
            embed(2, 3)
            residual(Part(0, 0))
            stats_h2(Part(0, 0))
            stats_h(2)
            ln_variance(2, LN_BOTH)
            maximum(Part(1, 1))
            ln_refine(2, LN_BOTH)
            ln_apply(LN_H, h, xn, xn_ready)
            subtract_max(Part(1, 1))
            apply_h2(0)

            def supertile(k, emb_next):
                p = Part(k, k)
                following = Part(k + 1, k + 1)
                take_v(k)
                take_xnT(k + 1)
                take_p(p)
                mask_p(p, (0, 1))
                mask_p(p, (2, 3))
                mask_p(p, (4, 5))
                take_q(k + 1)
                mask_q(k + 1, (0, 1))
                mask_q(k + 1, (2, 3))
                mask_q(k + 1, (4, 5))
                normalise(p)
                take_k(k + 1)
                take_x2T(k - 1)
                take_attnT(p)
                if emb_next:
                    embed(k + 2, 0)
                    embed(k + 2, 1)
                    embed(k + 2, 2)
                    embed(k + 2, 3)
                if not emb_next:
                    take_v(k + 1)
                residual(p)
                stats_h2(p)
                if emb_next:
                    stats_h(k + 2)
                ln_variance(k + 2, LN_BOTH if emb_next else LN_H2)
                if emb_next:
                    maximum(following)
                    ln_refine(k + 2, LN_BOTH)
                    ln_apply(LN_H, h, xn, xn_ready)
                    subtract_max(following)
                    apply_h2(k)
                if not emb_next:
                    for half in HALVES:
                        maximum(half)
                        subtract_max(half)

            with dve.Fori(1, SUPER - 2) as k:
                supertile(k, True)
            supertile(SUPER - 2, False)

            first, second = HALVES
            take_p(first)
            take_p(second)
            mask_p(first, (0, 1))
            mask_p(first, (2, 3))
            mask_p(first, (4, 5))
            mask_p(second, (0, 1))
            mask_p(second, (2, 3))
            mask_p(second, (4, 5))
            normalise(first)
            ln_refine(SUPER, LN_H2)
            apply_h2(SUPER - 2)
            normalise(second)
            take_attnT(first)
            take_attnT(second)
            residual(first)
            stats_h2(first)
            residual(second)
            stats_h2(second)
            ln_variance(SUPER + 1, LN_H2)
            take_x2T(SUPER - 2)
            ln_refine(SUPER + 1, LN_H2)
            apply_h2(SUPER - 1)
            take_x2T(SUPER - 1)

            sink = Chain(dve, sink_step, per=1)
            dve.wait_ge(logits_done, 1)
            dve.tensor_scalar(KA[:, :], bank[0][:, 0:P], 1 / UP, GATE_EPS, ALU.mult, ALU.max).then_inc(ka_ready, 1)
            with dve.Fori(0, SINKHORN_ITERS - 1) as n:
                sink.begin()
                dve.wait_ge(colsum_done, n + 1)
                sink.step(dve.reciprocal(cinv16[:, :], bank[2][:, 0:T]), n)
                dve.tensor_tensor(Cj[:, :], cinv16[:, :], row_of, ALU.mult).then_inc(c_ready, 1)
                dve.wait_ge(rowsum_done, n + 1)
                dve.reciprocal(R[:, :], bank[3][:, 0:T]).then_inc(r_ready, 1)
            tk = Chain(dve, top_step)
            dve.wait_ge(colsum_done, SINKHORN_ITERS)
            tk.step(dve.scalar_tensor_tensor(Cj[:, :], bank[2][:, 0:T], 1.0, row_of, ALU.mult, ALU.mult,
                                             accum_out=csum[:, :]))
            tk.step(dve.reciprocal(cinv[:, :], csum[:, :]))
            dve.tensor_scalar(scaled[:, :], all_of_row, cinv[:, 0:1], None, ALU.mult).then_inc(scaled_ready, 1)
            dve.wait_ge(rowsumB_done, 1)
            tk.step(dve.reciprocal(rinv[:, :], bank[3][:, 0:P]))
            tk.step(dve.scalar_tensor_tensor(G[:, :], KAT[:, :], cinv[:, 0:1], rinv[:, :], ALU.mult, ALU.mult))
            tk.step(dve.max(top[:, 0, :], G[:, :]))
            tk.step(dve.match_replace(G1[:, :], top[:, 0, :], G[:, :], -1.0))
            tk.step(dve.max(top[:, 1, :], G1[:, :]))
            tk.step(dve.match_replace(G2[:, :], top[:, 1, :], G1[:, :], -1.0))
            dve.tensor_scalar(M_bf[:, :], G2[:, :], 0.0, None, ALU.is_lt).then_inc(m_ready, 1)
            dve.wait_ge(m_ready, 1)
            tk.step(dve.tensor_tensor_scan(pos[:, :], M_bf[:, :], M_bf[:, :], 0.0, ALU.add, ALU.max))
            dve.wait_ge(later_done, 1)
            tk.step(dve.scalar_tensor_tensor(win[:, :], bank[4][:, 0:P], 0.0, M_bf[:, :], ALU.is_equal, ALU.mult))
            dve.tensor_tensor(slot[:, :], pos[:, :], win[:, :], ALU.mult).then_inc(slot_ready, 1)
            dve.scalar_tensor_tensor(wgate[:, :], G[:, :], 1 / UP, win[:, :], ALU.mult, ALU.mult).then_inc(wg_ready, 1)
            dve.wait_ge(slotT_done, 1)
            tk.step(dve.tensor_copy(slotT[:, :], bank[5][:, 0:P]))

            def one_hot(c):
                n = CHUNK * E
                dve.tensor_tensor(onehot[:, c * CHUNK:(c + 1) * CHUNK, :, :].rearrange("p b e j -> p (b e) j"),
                                  slotT[:, c * n:(c + 1) * n].unsqueeze(2).to_broadcast([P, n, CAP]),
                                  slot_no[:, :].unsqueeze(1).to_broadcast([P, n, CAP]),
                                  ALU.is_equal).then_inc(onehot_ready, 1)

            one_hot(0)
            dve.wait_ge(slotT_done, 2)
            dve.tensor_reduce(gate_tok[:, :], bank[6][:, 0:P].rearrange("p (b e) -> p b e", e=E), AX.X,
                              ALU.add).then_inc(gate_ready, 1)
            for step in range(NCH + 3):
                if step + 1 < NCH:
                    one_hot(step + 1)
                if step < NCH:
                    c = step
                    dve.wait_ge(xg_done, c + 1)
                    if c >= 2:
                        dve.wait_ge(yT_done, c - 1)
                    dve.tensor_copy(xg[1][:, c % 2, :, :, :].rearrange("p e b j -> p b e j"),
                                    bank[1][:, :].rearrange("p (b e j) -> p b e j", b=CHUNK, e=E)).then_inc(xg_lo, 1)
                if 2 <= step <= NCH + 1:
                    c = step - 2
                    low(y[1][:, c % 2, :, :], bank[Y_BANK[c % 2]][:, :].rearrange("p (b d) -> p b d", b=CHUNK),
                        y[0][:, c % 2, :, :], y_hi, c + 1, y_lo)
                if 3 <= step and step - 3 != ON_ACT:
                    c = step - 3
                    dve.wait_ge(scat_done, c + 1)
                    if c == 0:
                        dve.wait_ge(gate_ready, 1)
                        dve.wait_ge(h2s_in, 16)
                    for b in range(CHUNK):
                        row = c * CHUNK + b
                        ins = dve.scalar_tensor_tensor(res[:, row, :], bank[SCAT_BANK[c]][:, b * D:(b + 1) * D],
                                                       gate_tok[:, row:row + 1], h2s[:, row, :], ALU.mult, ALU.add)
                    ins.then_inc(res_ready[c], 1)


def _constants():
    import numpy as np
    c = np.zeros((P, C_ALL), np.float32)
    p = np.arange(P)
    c[:, C_IDENT:C_IDENT + P] = np.eye(P)
    c[p, C_GROUP + p // 16] = 1.0
    inv_freq = (1.0 / np.float32(10000.0) ** (np.arange(0, HD, 2, dtype=np.float32) / np.float32(HD))).astype(np.float32)
    angle = np.arange(T, dtype=np.float32)[:, None] * inv_freq[None, :]
    cos = np.cos(angle).astype(np.float32)
    sin = np.sin(angle).astype(np.float32)
    half = HD // 2
    d = p % HD
    c[:, C_COS:C_COS + T] = cos[:, d % half].T
    c[:, C_SIN:C_SIN + T] = (np.where(d < half, -1.0, 1.0)[None, :] * sin[:, d % half]).T
    c[:, C_ALL_OF_ROW:C_ALL_OF_ROW + P] = p[:, None] // E == p[None, :] // E
    c[:, C_ROW_OF:C_ROW_OF + T] = p[:, None] // E == np.arange(T)[None, :]
    c[:, C_LATER:C_LATER + P] = (p[:, None] // E == p[None, :] // E) & (p[:, None] > p[None, :])
    c[:, C_SLOT:C_SLOT + CAP] = np.arange(1, CAP + 1)
    rope = np.zeros((P, T, 32), np.float32)
    for g in range(P // HD):
        for d_in in range(HD):
            for t in range(T):
                row, base = g * HD + d_in, (g % 2) * HD
                rope[row, t, base + d_in] = cos[t, d_in % half]
                if d_in < half:
                    rope[row, t, base + d_in + half] = sin[t, d_in]
                else:
                    rope[row, t, base + d_in - half] = -sin[t, d_in - half]
    rope_hi = rope.astype(np.float16)
    rope = np.stack([rope_hi, (rope - rope_hi).astype(np.float16)], 1)
    pick = np.zeros((2 * T, 2, T, SPS), np.float16)
    for n in range(2):
        for t in range(T):
            pick[n * T + t, n, t, :] = 1.0
    edge = np.zeros((P, NG, T), np.float32)
    for n in range(NG):
        for s in range(S):
            start = s - (n + 2) // 2
            if start < 0 or start + n + 2 > S:
                edge[(s % SPT) * T:(s % SPT + 1) * T, n, s // SPT] = NO_ROW
    return c, rope, pick, edge


def kernel(x, L0_tok_emb_2, L0_tok_emb_3, L0_tok_emb_4, L0_tok_proj_w, L0_tok_proj_b, L0_attn_Wq, L0_attn_bq,
           L0_attn_Wk, L0_attn_bk, L0_attn_Wv, L0_attn_bv, L0_attn_Wo, L0_attn_bo, L0_ffn_gate_weight, L0_ffn_experts):
    import numpy as np
    import concourse.bacc as bacc
    from concourse.bass_utils import run_bass_kernel_spmd

    def swap_halves(b):
        return np.asarray(b).reshape(H, 2, HD // 2)[:, ::-1].reshape(D)

    proj = np.asarray(L0_tok_proj_w).reshape(D, NG, D).transpose(2, 1, 0).reshape(D, NG * D)
    weights = np.concatenate([
        proj, np.asarray(L0_attn_Wv).T, np.asarray(L0_attn_Wo).T, np.asarray(L0_attn_Wq), np.asarray(L0_attn_Wk),
        np.asarray(L0_ffn_gate_weight)[0],
        np.stack([np.asarray(L0_attn_bq), np.asarray(L0_attn_bk), swap_halves(L0_attn_bq), swap_halves(L0_attn_bk)], 1),
    ], axis=1)
    consts, rope, pick, edge = _constants()
    padded = np.pad(np.asarray(x), ((0, 0), (2, 1)))
    x_win = np.stack([padded[:, j:j + S].reshape(T, T, SPT).transpose(2, 0, 1).reshape(P, T) for j in range(WINDOW)], 1)
    arrays = {
        "x_win": x_win, "emb_2": np.asarray(L0_tok_emb_2), "emb_3": np.asarray(L0_tok_emb_3),
        "emb_4": np.asarray(L0_tok_emb_4), "weights": weights,
        "experts": np.asarray(L0_ffn_experts).transpose(1, 0, 2),
        "bias_rows": np.stack([np.asarray(L0_tok_proj_b), np.asarray(L0_attn_bv), np.asarray(L0_attn_bo)]),
        "consts": consts, "rope": rope, "pick": pick, "edge": edge,
    }
    arrays = {n: np.ascontiguousarray(a) for n, a in arrays.items()}
    nc = bacc.Bacc("TRN2", target_bir_lowering=False, num_devices=1)
    args = [nc.dram_tensor(n, a.shape, mybir.dt.from_np(a.dtype), kind="ExternalInput").ap() for n, a in arrays.items()]
    args.append(nc.dram_tensor("out", (T, S, D), F32, kind="ExternalOutput").ap())
    lm_layer(nc, *args)
    return run_bass_kernel_spmd(nc, [arrays], core_ids=[0]).results[0]["out"]
```
